# Optimizing a Trainium2 kernel written in Bass

```python
import numpy as np
import jax
import jax.numpy as jnp

def _softmax(x, axis=-1):
    return jax.nn.softmax(x, axis=axis)

def _gelu(x):
    return jax.nn.gelu(x, approximate=True)

def _silu(x):
    return jax.nn.silu(x)

def _sigmoid(x):
    return jax.nn.sigmoid(x)

def _layernorm(x, axis=-1, eps=1e-05):
    m = jnp.mean(x, axis=axis, keepdims=True)
    v = jnp.var(x, axis=axis, keepdims=True)
    return (x - m) / jnp.sqrt(v + eps)

def _scatter_add(tgt, idx, src, axis=0):
    return tgt.at[idx].add(src)

def _segment_sum(src, seg, n):
    return jax.ops.segment_sum(src, seg, n)
kernel_name = 'mk_rec_standalone_d1_rec_r8_69cc1f'

def setup_inputs(seed: int=0):
    np.random.seed(seed)
    _w = jnp.asarray

    def _rec_inputs():
        import jax
        import jax.numpy as jnp
        _rk = jax.random.key(seed)
        r_bottom_output = -0.000185639 + 0.999941 * jax.random.normal(jax.random.fold_in(_rk, 1), (2048, 27, 128), jnp.float32)
        r_bottom_mlp_output = -1.39393e-06 + 0.999914 * jax.random.normal(jax.random.fold_in(_rk, 2), (2048, 128), jnp.float32)
        return (r_bottom_output, r_bottom_mlp_output)
    r_bottom_output, r_bottom_mlp_output = _rec_inputs()

    def _L0_rec_setup():
        import jax, jax.numpy as jnp
        import numpy as np
        B, F, D = (4096, 27, 128)
        NUM_PAIRS = F * (F - 1) // 2
        NUM_INTER = D + NUM_PAIRS + 1
        MLP_SIZES = [1024, 1024, 512, 256]
        OUT_DIM = 1
        _TRIL_I, _TRIL_J = np.tril_indices(F, -1)

        def _interact(bottom_output, bottom_mlp_output):
            dots = jnp.einsum('bfd,bgd->bfg', bottom_output, bottom_output)
            pairs = dots[:, _TRIL_I, _TRIL_J]
            pad = jnp.zeros((bottom_mlp_output.shape[0], 1), bottom_mlp_output.dtype)
            return jnp.concatenate([bottom_mlp_output, pairs, pad], axis=1)
        key = jax.random.key(seed)
        ks = jax.random.split(key, 16)
        inp = {'bottom_output': jax.random.normal(ks[0], (B, F, D), jnp.float32), 'bottom_mlp_output': jax.random.normal(ks[1], (B, D), jnp.float32)}
        dims = [NUM_INTER] + MLP_SIZES
        k = 2
        for li in range(len(MLP_SIZES)):
            fan_in, fan_out = (dims[li], dims[li + 1])
            w = jax.random.normal(ks[k], (fan_out, fan_in), jnp.float32) / np.sqrt(fan_in)
            if li == 0:
                w = w.at[:, -1].set(0.0)
            inp[f'w{li}'] = w
            inp[f'b{li}'] = jnp.zeros((fan_out,), jnp.float32)
            k += 1
        inp['w_out'] = jax.random.normal(ks[k], (OUT_DIM, MLP_SIZES[-1]), jnp.float32) / np.sqrt(MLP_SIZES[-1])
        inp['b_out'] = jnp.zeros((OUT_DIM,), jnp.float32)
        return inp
    _L0_rec_all = _L0_rec_setup()
    _L0_rec_in = {k: v for k, v in _L0_rec_all.items() if k in ('w0', 'b0', 'w1', 'b1', 'w2', 'b2', 'w3', 'b3', 'w_out', 'b_out')}
    del _L0_rec_all
    return {'r_bottom_output': r_bottom_output, 'r_bottom_mlp_output': r_bottom_mlp_output, 'L0_rec_w0': _L0_rec_in['w0'], 'L0_rec_b0': _L0_rec_in['b0'], 'L0_rec_w1': _L0_rec_in['w1'], 'L0_rec_b1': _L0_rec_in['b1'], 'L0_rec_w2': _L0_rec_in['w2'], 'L0_rec_b2': _L0_rec_in['b2'], 'L0_rec_w3': _L0_rec_in['w3'], 'L0_rec_b3': _L0_rec_in['b3'], 'L0_rec_w_out': _L0_rec_in['w_out'], 'L0_rec_b_out': _L0_rec_in['b_out']}

def reference(r_bottom_output, r_bottom_mlp_output, L0_rec_w0, L0_rec_b0, L0_rec_w1, L0_rec_b1, L0_rec_w2, L0_rec_b2, L0_rec_w3, L0_rec_b3, L0_rec_w_out, L0_rec_b_out):
    import jax
    import jax.numpy as jnp

    def _L0_rec_ref(bottom_output, bottom_mlp_output, w0, b0, w1, b1, w2, b2, w3, b3, w_out, b_out):
        import jax, jax.numpy as jnp
        import numpy as np
        B, F, D = (4096, 27, 128)
        NUM_PAIRS = F * (F - 1) // 2
        NUM_INTER = D + NUM_PAIRS + 1
        MLP_SIZES = [1024, 1024, 512, 256]
        OUT_DIM = 1
        _TRIL_I, _TRIL_J = np.tril_indices(F, -1)

        def _interact(bottom_output, bottom_mlp_output):
            dots = jnp.einsum('bfd,bgd->bfg', bottom_output, bottom_output)
            pairs = dots[:, _TRIL_I, _TRIL_J]
            pad = jnp.zeros((bottom_mlp_output.shape[0], 1), bottom_mlp_output.dtype)
            return jnp.concatenate([bottom_mlp_output, pairs, pad], axis=1)
        x = _interact(bottom_output, bottom_mlp_output)
        for w, b in ((w0, b0), (w1, b1), (w2, b2), (w3, b3)):
            x = jax.nn.relu(x @ w.T + b)
        return x @ w_out.T + b_out
    y = _L0_rec_ref(r_bottom_output, r_bottom_mlp_output, L0_rec_w0, L0_rec_b0, L0_rec_w1, L0_rec_b1, L0_rec_w2, L0_rec_b2, L0_rec_w3, L0_rec_b3, L0_rec_w_out, L0_rec_b_out)
    return y

_drawn_inputs = setup_inputs


def setup_inputs(seed=0):
    import zlib

    import numpy as np

    out = dict(_drawn_inputs(seed))
    spreads = {'L0_rec_b0': (0.0, 0.8),
     'L0_rec_b1': (0.0, 0.8),
     'L0_rec_b2': (0.0, 0.761),
     'L0_rec_b3': (0.0, 0.678)}
    factors = {}
    for name, (base, spread) in spreads.items():
        noise = np.random.default_rng([zlib.crc32(name.encode()), seed]).standard_normal(out[name].shape)
        drawn = base * np.exp(spread * noise) if base else spread * noise
        out[name] = jnp.asarray(drawn.astype(out[name].dtype))
    for name, factor in factors.items():
        out[name] = (out[name] * factor).astype(out[name].dtype)
    return out
```

```python
from contextlib import ExitStack

import concourse.bass as bass
from concourse import mybir

F32 = mybir.dt.float32
F32R = mybir.dt.float32r
ALU = mybir.AluOpType
ACT = mybir.ActivationFunctionType

BATCH, FEATS, DIM = 2048, 27, 128
PAIRS = FEATS * (FEATS - 1) // 2
LAYERS = [(DIM + PAIRS + 1, 1024), (1024, 1024), (1024, 512), (512, 256)]
P = 128

CHUNK = 256
CHUNKS = BATCH // CHUNK
GROUP = 4
RUN = CHUNK // GROUP
GROUP_ROWS = GROUP * FEATS
QUAD = 32
UNIT_GROUPS = 4
UNIT_COLS = UNIT_GROUPS * GROUP_ROWS
UNITS = RUN // UNIT_GROUPS
LOAD_UNITS = 2
LOADS = UNITS // LOAD_UNITS

K_TILES = [-(-k // P) for k, _ in LAYERS]
M_TILES = [m // P for _, m in LAYERS]
TILE0 = [sum(K_TILES[j] * M_TILES[j] for j in range(n)) for n in range(5)]
K_LAST = LAYERS[0][0] - 3 * P
W0_GROUPS = TILE0[1] // 4
W_GROUPS = TILE0[4] // 4 + 1
RING = 4
RING_LOADS = 8 + 4 + 1

SLOTS = 24
OUT_SLOT, MLP_SLOT = 1, 21
FIRST_SLOT = [None, 9, 17, 22]
SPLITS = SLOTS - 1

ACC_RING, TURN_RING, GRAM_RING = 3, 1, 2
GRAM_BANKS = 2
assert ACC_RING + TURN_RING + GRAM_RING * GRAM_BANKS == 8 and SLOTS % ACC_RING == 0

HOOK = 12


def slot_of(layer, m):
    if layer == 0:
        return m if m == 0 else m + 1
    return FIRST_SLOT[layer] + m


def split_of(slot):
    return slot if slot <= OUT_SLOT else slot - 1


def gather_pieces():
    out = []
    for f in range(1, FEATS):
        g = 0
        while g < f:
            p = f * (f - 1) // 2 + g
            n = min(f - g, P - p % P)
            out.append((f, g, g + n, p // P, p % P))
            g += n
    return out


PIECES = gather_pieces()


def chunk_steps(gram):
    steps, done, unit = [], 0, 0

    def hook():
        nonlocal unit
        if gram and unit <= UNITS:
            if unit < UNITS:
                steps.append(("turn", unit))
            if unit > 0:
                steps.append(("gram", unit - 1))
            unit += 1

    for layer in range(4):
        if layer == 3 and gram:
            steps.append(("mlp",))
            steps.append(("pairs",))
        for m in range(M_TILES[layer]):
            k = 0
            while k < K_TILES[layer]:
                n = K_TILES[layer] - k
                if layer < 2:
                    n = min(n, (HOOK - done % HOOK) // 3)
                steps.append(("mm", layer, m, k, k + n))
                k += n
                done += 3 * n
                if layer < 2 and done % HOOK == 0:
                    hook()
            if layer == 0 and m == 0:
                steps.append(("out",))
    return steps


def dlrm_program(nc, x, x_mlp, w0, b0, w1, b1, w2, b2, w3, b3, w_out, b_out, y):
    weights = [w0, w1, w2, w3]
    biases = [b0, b1, b2, b3]
    with ExitStack() as ctx:
        def sb(name, shape, dt=F32):
            return ctx.enter_context(nc.sbuf_tensor(name, shape, dt))

        def sem(name):
            return ctx.enter_context(nc.semaphore(name))

        def shared(*specs):
            with ExitStack() as inner:
                return [inner.enter_context(nc.sbuf_tensor(n, s, F32)) for n, s in specs]

        w_hi = sb("w_hi", [P, TILE0[4] * P], F32R)
        w_lo = sb("w_lo", [P, TILE0[4] * P], F32R)
        x0 = sb("x0", [P, 4, 2, CHUNK], F32R)
        stage_w0, stage_small = shared(("stage_w0", [P, 8, LAYERS[0][0]]), ("stage_small", [P, P]))
        _, mlp_rows = shared(("under_mlp_rows", [P, 6 * 2 * CHUNK]), ("mlp_rows", [P, 2, P]))
        h_a = sb("h_a", [P, 8, 2, CHUNK], F32R)
        stage, = shared(("stage", [P, RING, 1024]))
        h_b = sb("h_b", [P, 8, 2, CHUNK], F32R)
        rows = sb("rows", [P, 2, LOAD_UNITS * UNIT_GROUPS, DIM])
        xt = sb("xt", [P, 2, UNIT_GROUPS, 2, GROUP * QUAD], F32R)
        half = sb("half", [P, 2, UNIT_GROUPS, QUAD])
        half_t = sb("half_t", [P, 2, UNIT_GROUPS, QUAD])
        grams = sb("grams", [P, FEATS, RUN])
        pairs = sb("pairs", [P, 3, CHUNK])
        ident = sb("ident", [P, P])
        h_full = sb("h_full", [P, 2, CHUNK])
        y_row = sb("y_row", [1, CHUNK])
        small_t = sb("small_t", [P, 24])
        wout_hi = sb("wout_hi", [P, 2], F32R)
        wout_lo = sb("wout_lo", [P, 2], F32R)
        bout = sb("bout", [1, 1])

        acc = ctx.enter_context(nc.psum_tensor("acc", [P, ACC_RING, 512], F32))
        turned_ps = ctx.enter_context(nc.psum_tensor("turned_ps", [P, TURN_RING, 512], F32))
        gram_ps = ctx.enter_context(nc.psum_tensor("gram_ps", [P, GRAM_RING * GRAM_BANKS, 512], F32))

        small_loaded = sem("small_loaded")
        w0_loaded = [sem(f"w0_loaded{i}") for i in range(2)]
        stage_loaded = [sem(f"stage_loaded{i}") for i in range(RING)]
        rows_loaded = [sem(f"rows_loaded{i}") for i in range(2)]
        mlp_loaded = sem("mlp_loaded")
        ident_ready = sem("ident_ready")
        pairs_zeroed = sem("pairs_zeroed")
        xt_zeroed = sem("xt_zeroed")
        half_zeroed = sem("half_zeroed")
        w_turned = sem("w_turned")
        w_hi_done = sem("w_hi_done")
        w_done = sem("w_done")
        turned = sem("turned")
        xt_hi_done = sem("xt_hi_done")
        xt_done = sem("xt_done")
        gram_done = sem("gram_done")
        half_hh = sem("half_hh")
        half_done = sem("half_done")
        half_turned = sem("half_turned")
        grams_done = sem("grams_done")
        spilled = sem("spilled")
        gathered = sem("gathered")
        pairs_hi_done = sem("pairs_hi_done")
        pairs_done = sem("pairs_done")
        filled = sem("filled")
        drained = sem("drained")
        split_done = sem("split_done")
        y_stored = sem("y_stored")

        x_view = x.rearrange("(c n j s) f d -> c n (s f) j d", n=LOADS, j=LOAD_UNITS * UNIT_GROUPS, s=GROUP)
        mlp_view = x_mlp.rearrange("(c t p) d -> c p t d", t=2, p=P)
        y_view = y.rearrange("(c n) o -> c o n", n=CHUNK)
        blocks = nc.dram_tensor("blocks", (FEATS, FEATS, CHUNK), F32).ap()

        def missing(c, slot):
            return 1 if isinstance(c, int) and c == CHUNKS - 1 and slot > MLP_SLOT else 0

        def slot_count(c, slot):
            return c * SLOTS + slot + 2 - missing(c, slot)

        def before_in_acc(c, slot):
            return slot_count(c, slot - ACC_RING) if slot >= ACC_RING else slot_count(c - 1, slot - ACC_RING + SLOTS)

        def split_count(c, slot):
            return c * SPLITS + split_of(slot) + 2 - missing(c, slot)

        def acc_slot(slot):
            return acc[:, slot % ACC_RING, 0:CHUNK]

        def out_tile(layer, m):
            if layer == 1:
                return h_b, m
            return h_a, m + (4 if layer == 3 else 0)

        def in_tile(layer, k, part):
            kk = K_LAST if layer == 0 and k == 3 else P
            src = x0 if layer == 0 else h_b if layer == 2 else h_a
            return src[0:kk, k, part, :]

        def weight(part, layer, m, k):
            kk = K_LAST if layer == 0 and k == 3 else P
            t = TILE0[layer] + m * K_TILES[layer] + k
            return part[0:kk, t * P:(t + 1) * P]

        def out_count(c):
            return slot_count(c + 1, OUT_SLOT) - (2 if isinstance(c, int) and c == CHUNKS - 1 else 0)

        def tile_of_group(g):
            return 4 * (g if g < W0_GROUPS else g - 1)

        def gram_in(u, s, part):
            b = u % GRAM_RING * GRAM_BANKS
            banks = gram_ps[QUAD * s:QUAD * s + FEATS, b:b + GRAM_BANKS, :]
            at = part * P + s * QUAD
            return banks.rearrange("p a (b c) -> p a b c", b=2)[:, :, :, at:at + FEATS]

        def half_out(u, s):
            return half[QUAD * s:QUAD * s + FEATS, u % 2].rearrange("p (a b) g -> p a b g", a=2)[:, :, :, 0:FEATS]

        def cols(ap):
            return ap.rearrange("p (s i) -> p s i", s=GROUP)

        def by_sample(ap):
            return ap.rearrange("p (i s) -> p s i", s=GROUP)

        block = ctx.enter_context(nc.Block())

        @block.sync
        def _(sp):
            def load_rows(d, n):
                if isinstance(d, int) and d == 0 and n < 2:
                    pass
                else:
                    sp.wait_ge(turned, d * UNITS + (n - 1) * LOAD_UNITS)
                sp.dma_start(rows[0:GROUP_ROWS, n % 2], x_view[d, n]).then_inc(rows_loaded[n % 2], 16)

            def load_stage(n):
                if n >= RING:
                    sp.wait_ge(w_turned, W0_GROUPS + 1 + 2 * (n - RING + 1))
                if n < 12:
                    w, m = (w1, n) if n < 8 else (w2, n - 8)
                    sp.dma_start(stage[:, n % RING, :], w[m * P:(m + 1) * P, :]).then_inc(stage_loaded[n % RING], 16)
                else:
                    sp.dma_start(stage[:, n % RING, :].rearrange("p (m k) -> p m k", m=2),
                                 w3.rearrange("(m p) k -> p m k", p=P)).then_inc(stage_loaded[n % RING], 16)

            def gather(d):
                if isinstance(d, int) and d == 0:
                    sp.wait_ge(pairs_zeroed, 1)
                sp.wait_ge(grams_done, d * UNITS + UNITS)
                for s in range(GROUP):
                    sp.dma_start(blocks[:, :, s * RUN:(s + 1) * RUN],
                                 grams[QUAD * s:QUAD * s + FEATS, :, :]).then_inc(spilled, 16)
                sp.wait_ge(spilled, (d + 1) * GROUP * 16)
                for f, g0, g1, tile, p0 in PIECES:
                    sp.dma_start(pairs[p0:p0 + g1 - g0, tile], blocks[f, g0:g1]).then_inc(gathered, 16)

            def load_mlp(d):
                sp.dma_start(mlp_rows[:, :, :], mlp_view[d]).then_inc(mlp_loaded, 16)

            def store_y(c):
                sp.wait_ge(drained, out_count(c))
                sp.dma_start(y_view[c], y_row[:, :]).then_inc(y_stored, 16)

            def chunk(c):
                for n in range(2, LOADS):
                    load_rows(c + 1, n)
                    if n == 4 and not (isinstance(c, int) and c == 0):
                        store_y(c - 1)
                gather(c + 1)
                if not (isinstance(c, int) and c == CHUNKS - 2):
                    for n in range(2):
                        load_rows(c + 2, n)
                sp.wait_ge(filled, slot_count(c, slot_of(1, 7)))
                load_mlp(c + 1)

            w0_view = w0.rearrange("(m p) k -> p m k", p=P)
            for i in range(2):
                sp.dma_start(stage_w0[:, 4 * i:4 * i + 4, :], w0_view[:, 4 * i:4 * i + 4]).then_inc(w0_loaded[i], 16)
                load_rows(0, i)
            r = 0
            for b, m in zip(biases + [w_out], M_TILES + [2]):
                src = b.rearrange("o (m p) -> (o m) p", p=P) if b is w_out else b.rearrange("(m p) -> m p", p=P)
                sp.dma_start(stage_small[r:r + m, :], src).then_inc(small_loaded, 16)
                r += m
            sp.dma_start(bout[:, :], b_out.rearrange("(o n) -> o n", o=1)).then_inc(small_loaded, 16)
            for n in range(RING_LOADS - 1):
                load_stage(n)
                if n + 2 < LOADS:
                    load_rows(0, n + 2)
            gather(0)
            load_stage(RING_LOADS - 1)
            sp.wait_ge(w_turned, W0_GROUPS + 1)
            load_mlp(0)
            for n in range(2):
                load_rows(1, n)
            chunk(0)
            with sp.Fori(1, CHUNKS - 2) as c:
                chunk(c)
            chunk(CHUNKS - 2)
            store_y(CHUNKS - 2)
            store_y(CHUNKS - 1)
            sp.wait_ge(y_stored, 16 * CHUNKS)

        @block.gpsimd
        def _(pool):
            nc.gpsimd.memset(ident[:], 0.0).then_inc(ident_ready, 1)
            pool.wait_ge(ident_ready, 1)
            nc.gpsimd.affine_select(out=ident[:], in_=ident[:], compare_op=ALU.not_equal, fill=1.0, base=0,
                                    pattern=[[-1, P]], channel_multiplier=1).then_inc(ident_ready, 1)
            nc.gpsimd.memset(pairs[:], 0.0).then_inc(pairs_zeroed, 1)

        @block.tensor
        def _(pe):
            def turn_weights(g):
                bank = g % 2
                if g >= 2:
                    pe.wait_ge(w_done, g - 1)
                if g < W0_GROUPS:
                    if g % 4 == 0:
                        pe.wait_ge(w0_loaded[g // 4], 16)
                    for k in range(4):
                        kk = K_LAST if k == 3 else P
                        last = nc.tensor.transpose(acc[0:kk, bank, k * P:(k + 1) * P],
                                                   stage_w0[:, g, k * P:k * P + kk], ident[:])
                elif g == W0_GROUPS:
                    pe.wait_ge(small_loaded, 6 * 16)
                    last = nc.tensor.transpose(acc[:, bank, 0:24], stage_small[0:24, :], ident[0:24, 0:24])
                else:
                    n, part = (g - W0_GROUPS - 1) // 2, (g - W0_GROUPS - 1) % 2
                    if part == 0:
                        pe.wait_ge(stage_loaded[n % RING], 16 * (n // RING + 1))
                    for k in range(4):
                        at = (4 * part + k) * P
                        last = nc.tensor.transpose(acc[:, bank, k * P:(k + 1) * P],
                                                   stage[:, n % RING, at:at + P], ident[:])
                last.then_inc(w_turned, 1)

            def turn(d, u):
                n = u // LOAD_UNITS
                if u % LOAD_UNITS == 0:
                    pe.wait_ge(rows_loaded[n % 2], (d * (LOADS // 2) + n // 2 + 1) * 16)
                if not (isinstance(d, int) and d == 0 and u < TURN_RING):
                    pe.wait_ge(xt_done, d * UNITS + u + 1 - TURN_RING)
                for j in range(UNIT_GROUPS):
                    last = nc.tensor.transpose(turned_ps[:, u % TURN_RING, j * GROUP_ROWS:(j + 1) * GROUP_ROWS],
                                               rows[0:GROUP_ROWS, n % 2, u % LOAD_UNITS * UNIT_GROUPS + j, :],
                                               ident[0:GROUP_ROWS, 0:GROUP_ROWS])
                last.then_inc(turned, 1)

            def gram(d, u):
                pe.wait_ge(xt_done, d * UNITS + u + 1)
                if not (isinstance(d, int) and d == 0 and u < GRAM_RING):
                    pe.wait_ge(half_done, d * UNITS + u + 1 - GRAM_RING)
                for j in range(UNIT_GROUPS):
                    at = j % 2 * 2 * P
                    last = nc.tensor.matmul(gram_ps[:, u % GRAM_RING * GRAM_BANKS + j // 2, at:at + 2 * P], xt[:, u % 2, j, 0, :],
                                            xt[:, u % 2, j].rearrange("p h n -> p (h n)"), start=True, stop=True)
                last.then_inc(gram_done, 1)

            def turn_mlp(slot):
                for t in range(2):
                    last = nc.tensor.transpose(acc_slot(slot)[:, t * P:(t + 1) * P], mlp_rows[:, t, :], ident[:])
                return last

            def products(c, layer, m, k0, k1):
                slot = slot_of(layer, m)
                if k0 == 0:
                    if isinstance(c, int) and c == 0 and slot < ACC_RING - 1:
                        pe.wait_ge(w_done, W_GROUPS)
                    else:
                        pe.wait_ge(drained, before_in_acc(c, slot))
                if layer == 0 and m == 0:
                    if k0 == 0:
                        pe.wait_ge(pairs_done, c + 1)
                        pe.wait_ge(split_done, 1 if isinstance(c, int) and c == 0 else split_count(c - 1, MLP_SLOT))
                for k in range(k0, k1):
                    if layer > 0 and m == 0:
                        pe.wait_ge(split_done, split_count(c, slot_of(layer - 1, k)))
                    for n, (wp, xp) in enumerate(((w_hi, 0), (w_hi, 1), (w_lo, 0))):
                        last = nc.tensor.matmul(acc_slot(slot), weight(wp, layer, m, k), in_tile(layer, k, xp),
                                                start=(k == 0 and n == 0), stop=(k == K_TILES[layer] - 1 and n == 2))
                if k1 == K_TILES[layer]:
                    last.then_inc(filled, 2 if isinstance(c, int) and c == 0 and slot == 0 else 1)

            def out_row(c):
                pe.wait_ge(split_done, split_count(c, slot_of(3, 1)))
                pe.wait_ge(drained, before_in_acc(c + 1, OUT_SLOT))
                for k in range(2):
                    for n, (wp, xp) in enumerate(((wout_hi, 0), (wout_hi, 1), (wout_lo, 0))):
                        last = nc.tensor.matmul(acc_slot(OUT_SLOT)[0:1], wp[:, k:k + 1], h_a[:, 4 + k, xp, :],
                                                start=(k == 0 and n == 0), stop=(k == 1 and n == 2))
                last.then_inc(filled, 1)

            def chunk(c):
                ends = isinstance(c, int) and c == CHUNKS - 1
                for step in chunk_steps(not ends):
                    if step[0] == "mm":
                        products(c, *step[1:])
                    elif step[0] == "turn":
                        turn(c + 1, step[1])
                    elif step[0] == "gram":
                        gram(c + 1, step[1])
                    elif step[0] == "out" and not (isinstance(c, int) and c == 0):
                        out_row(c - 1)
                    elif step[0] == "mlp":
                        pe.wait_ge(mlp_loaded, (c + 2) * 16)
                        pe.wait_ge(drained, before_in_acc(c, MLP_SLOT))
                        turn_mlp(MLP_SLOT).then_inc(filled, 1)

            pe.wait_ge(ident_ready, 2)
            for g in range(W0_GROUPS + 1):
                turn_weights(g)
            for u in range(UNITS + 1):
                if u < UNITS:
                    turn(0, u)
                    turn_weights(W0_GROUPS + 1 + u)
                if u > 0:
                    gram(0, u - 1)
            for g in range(W0_GROUPS + 1 + UNITS, W_GROUPS):
                turn_weights(g)
            pe.wait_ge(w_done, W_GROUPS)
            pe.wait_ge(mlp_loaded, 16)
            turn_mlp(SLOTS - 1).then_inc(filled, 1)
            chunk(0)
            with pe.Fori(1, CHUNKS - 1) as c:
                chunk(c)
            chunk(CHUNKS - 1)
            out_row(CHUNKS - 1)

        @block.scalar
        def _(act):
            def weights_hi(g):
                act.wait_ge(w_turned, g + 1)
                t = tile_of_group(g)
                if g == W0_GROUPS:
                    nc.scalar.activation(small_t[:], acc[:, g % 2, 0:24], ACT.Copy)
                    last = nc.scalar.activation(wout_hi[:], acc[:, g % 2, 22:24], ACT.Copy)
                elif g < W0_GROUPS:
                    nc.scalar.activation(w_hi[:, t * P:(t + 3) * P], acc[:, g % 2, 0:3 * P], ACT.Copy)
                    last = nc.scalar.activation(w_hi[0:K_LAST, (t + 3) * P:(t + 4) * P],
                                                acc[0:K_LAST, g % 2, 3 * P:4 * P], ACT.Copy)
                else:
                    last = nc.scalar.activation(w_hi[:, t * P:(t + 4) * P], acc[:, g % 2, :], ACT.Copy)
                last.then_inc(w_hi_done, 1)

            def turned_hi(d, u):
                act.wait_ge(turned, d * UNITS + u + 1)
                if isinstance(d, int) and d == 0 and u < 2:
                    act.wait_ge(xt_zeroed, 1)
                else:
                    act.wait_ge(gram_done, d * UNITS + u - 1)
                nc.scalar.activation(
                    xt[:, u % 2, :, 0, :].rearrange("p j (s f) -> p j s f", s=GROUP)[:, :, :, 0:FEATS],
                    turned_ps[:, u % TURN_RING, 0:UNIT_COLS].rearrange("p (j s f) -> p j s f", s=GROUP, f=FEATS),
                    ACT.Copy).then_inc(xt_hi_done, 1)

            def gram_hh(d, u):
                act.wait_ge(gram_done, d * UNITS + u + 1)
                if not (isinstance(d, int) and d == 0 and u < 2):
                    act.wait_ge(grams_done, d * UNITS + u - 1)
                else:
                    act.wait_ge(half_zeroed, 1)
                for s in range(GROUP):
                    last = nc.scalar.activation(half_out(u, s), gram_in(u, s, 0), ACT.Copy, scale=0.5)
                last.then_inc(half_hh, 1)

            def drain(c, slot, full, high, src, func, **kw):
                act.wait_ge(filled, slot_count(c, slot))
                if slot == 2 or slot > 3:
                    act.wait_ge(split_done, split_count(c, slot - 2))
                elif slot == 3 and isinstance(c, int) and c == 0:
                    act.wait_ge(split_done, 1)
                elif not (isinstance(c, int) and c == 0):
                    act.wait_ge(split_done, split_count(c - 1, SLOTS - 2 if slot == 0 else SLOTS - 1))
                nc.scalar.activation(full, src, func, **kw)
                nc.scalar.activation(high, src, func, **kw).then_inc(
                    drained, 2 if isinstance(c, int) and c == 0 and slot == 0 else 1)

            def pairs_hi(d):
                act.wait_ge(gathered, (d + 1) * 16 * len(PIECES))
                nc.scalar.activation(x0[:, 1:4, 0, :], pairs[:], ACT.Copy).then_inc(pairs_hi_done, 1)

            def out_row(c):
                act.wait_ge(filled, out_count(c))
                if not (isinstance(c, int) and c == 0):
                    act.wait_ge(y_stored, c * 16)
                nc.scalar.activation(by_sample(y_row[:, :]), cols(acc_slot(OUT_SLOT)[0:1]), ACT.Identity,
                                     bias=bout[:, :]).then_inc(drained, 1)

            def chunk(c):
                ends = isinstance(c, int) and c == CHUNKS - 1
                for step in chunk_steps(not ends):
                    if step[0] == "mm":
                        _, layer, m, _, k1 = step
                        if k1 == K_TILES[layer]:
                            h, t = out_tile(layer, m)
                            bias = small_t[:, sum(M_TILES[:layer]) + m:sum(M_TILES[:layer]) + m + 1]
                            slot = slot_of(layer, m)
                            drain(c, slot, h_full[:, slot % 2, :], h[:, t, 0, :], acc_slot(slot), ACT.Relu, bias=bias)
                    elif step[0] == "turn":
                        turned_hi(c + 1, step[1])
                    elif step[0] == "gram":
                        gram_hh(c + 1, step[1])
                    elif step[0] == "mlp":
                        drain(c, MLP_SLOT, cols(h_full[:, MLP_SLOT % 2, :]), cols(x0[:, 0, 0, :]),
                              by_sample(acc_slot(MLP_SLOT)), ACT.Copy)
                    elif step[0] == "pairs":
                        pairs_hi(c + 1)
                    elif step[0] == "out" and not (isinstance(c, int) and c == 0):
                        out_row(c - 1)

            for g in range(W0_GROUPS + 1):
                weights_hi(g)
            for u in range(UNITS + 1):
                if u < UNITS:
                    turned_hi(0, u)
                    weights_hi(W0_GROUPS + 1 + u)
                if u > 0:
                    gram_hh(0, u - 1)
            for g in range(W0_GROUPS + 1 + UNITS, W_GROUPS):
                weights_hi(g)
            act.wait_ge(filled, 1)
            nc.scalar.activation(cols(h_full[:, 1, :]), by_sample(acc_slot(SLOTS - 1)), ACT.Copy)
            nc.scalar.activation(cols(x0[:, 0, 0, :]), by_sample(acc_slot(SLOTS - 1)), ACT.Copy).then_inc(drained, 1)
            pairs_hi(0)
            chunk(0)
            with act.Fori(1, CHUNKS - 1) as c:
                chunk(c)
            chunk(CHUNKS - 1)
            out_row(CHUNKS - 1)

        @block.vector
        def _(dve):
            def weights_lo(g):
                dve.wait_ge(w_hi_done, g + 1)
                t = tile_of_group(g)
                if g == W0_GROUPS:
                    last = nc.vector.tensor_tensor(wout_lo[:], acc[:, g % 2, 22:24], wout_hi[:].bitcast(F32), ALU.subtract)
                elif g < W0_GROUPS:
                    a, b = t * P, (t + 3) * P
                    nc.vector.tensor_tensor(w_lo[:, a:b], acc[:, g % 2, 0:3 * P], w_hi[:, a:b].bitcast(F32), ALU.subtract)
                    a, b = b, b + P
                    last = nc.vector.tensor_tensor(w_lo[0:K_LAST, a:b], acc[0:K_LAST, g % 2, 3 * P:4 * P],
                                                   w_hi[0:K_LAST, a:b].bitcast(F32), ALU.subtract)
                else:
                    a, b = t * P, (t + 4) * P
                    last = nc.vector.tensor_tensor(w_lo[:, a:b], acc[:, g % 2, :], w_hi[:, a:b].bitcast(F32), ALU.subtract)
                last.then_inc(w_done, 1)

            def turned_lo(d, u):
                dve.wait_ge(xt_hi_done, d * UNITS + u + 1)
                hi, lo = (xt[:, u % 2, :, h, :].rearrange("p j (s f) -> p j s f", s=GROUP)[:, :, :, 0:FEATS]
                          for h in range(2))
                nc.vector.tensor_tensor(
                    lo, turned_ps[:, u % TURN_RING, 0:UNIT_COLS].rearrange("p (j s f) -> p j s f", s=GROUP, f=FEATS),
                    hi.bitcast(F32), ALU.subtract).then_inc(xt_done, 1)

            def gram_sum(d, u):
                n = d * UNITS + u + 1
                dve.wait_ge(half_hh, n)
                for s in range(GROUP):
                    last = nc.vector.tensor_tensor(half_out(u, s), gram_in(u, s, 1), half_out(u, s), ALU.add)
                last.then_inc(half_done, 1)
                dve.wait_ge(half_done, n)
                nc.vector.transpose(half_t[:, u % 2].rearrange("p j g -> p (j g)"),
                                    half[:, u % 2].rearrange("p j g -> p (j g)")).then_inc(half_turned, 1)
                dve.wait_ge(half_turned, n)
                if not (isinstance(d, int) and d == 0) and u == 0:
                    dve.wait_ge(spilled, d * GROUP * 16)
                nc.vector.tensor_tensor(
                    grams[:, :, u * UNIT_GROUPS:(u + 1) * UNIT_GROUPS].rearrange("p g j -> p j g"),
                    half[:, u % 2, :, 0:FEATS], half_t[:, u % 2, :, 0:FEATS], ALU.add).then_inc(grams_done, 1)

            def low(c, slot, h, t):
                dve.wait_ge(drained, slot_count(c, slot))
                nc.vector.tensor_tensor(h[:, t, 1, :], h_full[:, slot % 2, :], h[:, t, 0, :].bitcast(F32),
                                        ALU.subtract).then_inc(split_done, 1)

            def pairs_lo(d):
                dve.wait_ge(pairs_hi_done, d + 1)
                nc.vector.tensor_tensor(x0[:, 1:4, 1, :], pairs[:], x0[:, 1:4, 0, :].bitcast(F32),
                                        ALU.subtract).then_inc(pairs_done, 1)

            def chunk(c):
                ends = isinstance(c, int) and c == CHUNKS - 1
                for step in chunk_steps(not ends):
                    if step[0] == "mm":
                        _, layer, m, _, k1 = step
                        if k1 == K_TILES[layer]:
                            low(c, slot_of(layer, m), *out_tile(layer, m))
                    elif step[0] == "turn":
                        turned_lo(c + 1, step[1])
                    elif step[0] == "gram":
                        gram_sum(c + 1, step[1])
                    elif step[0] == "mlp":
                        low(c, MLP_SLOT, x0, 0)
                    elif step[0] == "pairs":
                        pairs_lo(c + 1)

            nc.vector.memset(xt[:].bitcast(F32), 0.0).then_inc(xt_zeroed, 1)
            nc.vector.memset(half[:], 0.0).then_inc(half_zeroed, 1)
            for g in range(W0_GROUPS + 1):
                weights_lo(g)
            for u in range(UNITS + 1):
                if u < UNITS:
                    turned_lo(0, u)
                    weights_lo(W0_GROUPS + 1 + u)
                if u > 0:
                    gram_sum(0, u - 1)
            for g in range(W0_GROUPS + 1 + UNITS, W_GROUPS):
                weights_lo(g)
            dve.wait_ge(drained, 1)
            nc.vector.tensor_tensor(x0[:, 0, 1, :], h_full[:, 1, :], x0[:, 0, 0, :].bitcast(F32),
                                    ALU.subtract).then_inc(split_done, 1)
            pairs_lo(0)
            chunk(0)
            with dve.Fori(1, CHUNKS - 1) as c:
                chunk(c)
            chunk(CHUNKS - 1)


_INS = ['r_bottom_output', 'r_bottom_mlp_output', 'L0_rec_w0', 'L0_rec_b0', 'L0_rec_w1', 'L0_rec_b1', 'L0_rec_w2',
        'L0_rec_b2', 'L0_rec_w3', 'L0_rec_b3', 'L0_rec_w_out', 'L0_rec_b_out']
_OUTS = [((2048, 1), 'float32')]


def kernel(**inputs):
    import numpy as _np
    import concourse.bacc as _bacc
    from concourse import mybir as _mybir
    from concourse.bass_utils import run_bass_kernel_spmd as _run

    nc = _bacc.Bacc("TRN2", target_bir_lowering=False, num_devices=1)
    arrays, args = {}, []
    for name in _INS:
        a = _np.ascontiguousarray(inputs[name])
        arrays[f"in_{name}_dram"] = a
        args.append(nc.dram_tensor(f"in_{name}_dram", a.shape, _mybir.dt.from_np(a.dtype), kind="ExternalInput").ap())
    for i, (shape, dtype) in enumerate(_OUTS):
        dt = _mybir.dt.from_np(_np.dtype(dtype))
        args.append(nc.dram_tensor(f"out_{i}_dram", shape, dt, kind="ExternalOutput").ap())
    dlrm_program(nc, *args)
    r = _run(nc, [arrays], core_ids=[0])
    return r.results[0]["out_0_dram"]
```

```python
from contextlib import ExitStack

import concourse.bass as bass
from concourse import mybir

F32 = mybir.dt.float32
F32R = mybir.dt.float32r
ALU = mybir.AluOpType
ACT = mybir.ActivationFunctionType

BATCH, FEATS, DIM = 2048, 27, 128
PAIRS = FEATS * (FEATS - 1) // 2
LAYERS = [(DIM + PAIRS + 1, 1024), (1024, 1024), (1024, 512), (512, 256)]
P = 128

CHUNK = 256
CHUNKS = BATCH // CHUNK
GROUP = 4
RUN = CHUNK // GROUP
GROUP_ROWS = GROUP * FEATS
QUAD = 32
UNIT_GROUPS = 4
UNIT_COLS = UNIT_GROUPS * GROUP_ROWS
UNITS = RUN // UNIT_GROUPS
ROWS_RING = 4

K_TILES = [-(-k // P) for k, _ in LAYERS]
M_TILES = [m // P for _, m in LAYERS]
TILE0 = [sum(K_TILES[j] * M_TILES[j] for j in range(n)) for n in range(5)]
K_LAST = LAYERS[0][0] - 3 * P
W0_GROUPS = TILE0[1] // 4
W_GROUPS = TILE0[4] // 4 + 1
W1_HEAD, W0_ALL, SMALL = list(range(9, 17)), list(range(W0_GROUPS)), [W0_GROUPS]
W1_TAIL, W2_ALL, W3_ALL = list(range(17, 25)), list(range(25, 33)), list(range(33, 35))
ORDER = W1_HEAD[:2] + W0_ALL[:4] + W1_HEAD[2:] + W0_ALL[4:] + SMALL + W2_ALL + W3_ALL + W1_TAIL
BETWEEN_UNITS, FIRST_BETWEEN = 12, 5

SLOTS = 24
OUT_SLOT, MLP_SLOT = 1, 21
FIRST_SLOT = [None, 9, 17, 22]
SPLITS = SLOTS - 1

ACC_RING, TURN_RING, GRAM_RING = 2, 2, 2
GRAM_BANKS = 2
XT_RING, XT_LAG = 4, 2
assert ACC_RING + TURN_RING + GRAM_RING * GRAM_BANKS == 8 and SLOTS % ACC_RING == 0

HOOK = 9


def slot_of(layer, m):
    if layer == 0:
        return m if m == 0 else m + 1
    return FIRST_SLOT[layer] + m


def split_of(slot):
    return slot if slot <= OUT_SLOT else slot - 1


BAND = [14 if f < 13 else 13 for f in range(FEATS - 1)]
BAND0 = [sum(BAND[:f]) for f in range(FEATS)]
assert BAND0[-1] == PAIRS


def band_pieces():
    out, q = [], 0
    while q < PAIRS:
        f = max(f for f in range(FEATS - 1) if BAND0[f] <= q)
        room = P - q % P
        k, whole = q - BAND0[f] + 1, 1
        n = min(BAND[f] + 1 - k, room)
        if k == 1 and n == BAND[f]:
            while f + whole < FEATS - 1 and BAND[f + whole] == n and (whole + 1) * n <= room:
                whole += 1
        out.append((f, whole, k, n, q))
        q += whole * n
    return out


PIECES = band_pieces()


def band_of_rows():
    out = []
    for a in range(1, FEATS):
        place = []
        for b in range(a):
            flat = min(x for x in (b * FEATS + a, a * FEATS + b) if 1 <= x % (FEATS + 1) <= BAND[x // (FEATS + 1)])
            place.append(BAND0[flat // (FEATS + 1)] + flat % (FEATS + 1) - 1)
        b = 0
        while b < a:
            n = 1
            while b + n < a and place[b + n] - place[b + n - 1] == (place[b + 1] - place[b]) > 0:
                n += 1
            out.append((a * (a - 1) // 2 + b, n, place[b], place[b + 1] - place[b] if n > 1 else 1))
            b += n
    return out


ROW_RUNS = band_of_rows()
assert sorted(q + i * d for _, n, q, d in ROW_RUNS for i in range(n)) == list(range(PAIRS))

def chunk_steps(gram):
    steps, done, unit = [], 0, 0

    def hook():
        nonlocal unit
        if gram and unit < UNITS + XT_LAG:
            if unit < UNITS:
                steps.append(("turn", unit))
            if unit >= XT_LAG:
                steps.append(("gram", unit - XT_LAG))
            unit += 1

    for layer in range(4):
        if layer == 3 and gram:
            steps.append(("mlp",))
            steps.append(("pairs",))
        for m in range(M_TILES[layer]):
            k = 0
            while k < K_TILES[layer]:
                n = K_TILES[layer] - k
                if layer < 2:
                    n = min(n, (HOOK - done % HOOK) // 3)
                steps.append(("mm", layer, m, k, k + n))
                k += n
                done += 3 * n
                if layer < 2 and done % HOOK == 0:
                    hook()
            if layer == 0 and m == 0:
                steps.append(("out",))
    return steps


def dlrm_program(nc, x, x_mlp, w0, b0, w1, b1, w2, b2, w3, b3, w_out, b_out, y):
    weights = [w0, w1, w2, w3]
    biases = [b0, b1, b2, b3]
    with ExitStack() as ctx:
        def sb(name, shape, dt=F32):
            return ctx.enter_context(nc.sbuf_tensor(name, shape, dt))

        def sem(name):
            return ctx.enter_context(nc.semaphore(name))

        def shared(*specs):
            with ExitStack() as inner:
                return [inner.enter_context(nc.sbuf_tensor(n, s, F32)) for n, s in specs]

        w_hi = sb("w_hi", [P, TILE0[4] * P], F32R)
        w_lo = sb("w_lo", [P, TILE0[4] * P], F32R)
        w0_ordered, = shared(("w0_ordered", [P, 4, PAIRS + 1]))
        x0 = sb("x0", [P, 4, 2, CHUNK], F32R)
        stage_w0, = shared(("stage_w0", [P, 8, LAYERS[0][0]]))
        stage_a, = shared(("stage_a", [P, 4, 1024]))
        h_a = sb("h_a", [P, 8, 2, CHUNK], F32R)
        stage_b, = shared(("stage_b", [P, 4, 1024]))
        h_b = sb("h_b", [P, 8, 2, CHUNK], F32R)
        stage_w3 = sb("stage_w3", [P, 2, 512])
        stage_small = sb("stage_small", [24, P])
        rows = sb("rows", [P, ROWS_RING, UNIT_GROUPS, DIM])
        mlp_rows = sb("mlp_rows", [P, 2, P])
        xt = sb("xt", [P, XT_RING, UNIT_GROUPS, 2, GROUP * QUAD], F32R)
        parts = sb("parts", [P, 2, 2, UNIT_GROUPS, QUAD])
        low_t = sb("low_t", [P, UNIT_GROUPS, QUAD])
        grams = sb("grams", [P, FEATS, RUN])
        pairs = sb("pairs", [P, 3, CHUNK])
        ident = sb("ident", [P, P])
        h_full = sb("h_full", [P, 2, CHUNK])
        y_row = sb("y_row", [1, CHUNK])
        small_t = sb("small_t", [P, 24])
        wout_hi = sb("wout_hi", [P, 2], F32R)
        wout_lo = sb("wout_lo", [P, 2], F32R)
        bout = sb("bout", [1, 1])

        acc = ctx.enter_context(nc.psum_tensor("acc", [P, ACC_RING, 512], F32))
        turned_ps = ctx.enter_context(nc.psum_tensor("turned_ps", [P, TURN_RING, 512], F32))
        gram_ps = ctx.enter_context(nc.psum_tensor("gram_ps", [P, GRAM_RING * GRAM_BANKS, 512], F32))

        small_loaded = sem("small_loaded")
        w0_loaded = [sem(f"w0_loaded{i}") for i in range(2)]
        w0_in_order = sem("w0_in_order")
        w1_head_loaded = sem("w1_head_loaded")
        w1_tail_loaded = sem("w1_tail_loaded")
        w2_loaded = sem("w2_loaded")
        w3_loaded = sem("w3_loaded")
        rows_loaded = [sem(f"rows_loaded{i}") for i in range(ROWS_RING)]
        mlp_loaded = sem("mlp_loaded")
        ident_ready = sem("ident_ready")
        pairs_zeroed = sem("pairs_zeroed")
        xt_zeroed = sem("xt_zeroed")
        parts_zeroed = sem("parts_zeroed")
        w_turned = sem("w_turned")
        w_hi_done = sem("w_hi_done")
        w_done = sem("w_done")
        turned = sem("turned")
        xt_hi_done = sem("xt_hi_done")
        xt_done = sem("xt_done")
        gram_done = sem("gram_done")
        parts_done = sem("parts_done")
        low_turned = sem("low_turned")
        sum_done = sem("sum_done")
        grams_done = sem("grams_done")
        spilled = sem("spilled")
        gathered = sem("gathered")
        pairs_hi_done = sem("pairs_hi_done")
        pairs_done = sem("pairs_done")
        filled = sem("filled")
        drained = sem("drained")
        high_done = sem("high_done")
        split_done = sem("split_done")
        y_stored = sem("y_stored")

        x_view = x.rearrange("(c u j s) f d -> c u (s f) j d", u=UNITS, j=UNIT_GROUPS, s=GROUP)
        mlp_view = x_mlp.rearrange("(c t p) d -> c p t d", t=2, p=P)
        y_view = y.rearrange("(c n) o -> c o n", n=CHUNK)
        blocks = nc.dram_tensor("blocks", (FEATS, FEATS, CHUNK), F32).ap()
        flat_blocks = blocks.rearrange("f g n -> (f g) n")

        def missing(c, slot):
            return 1 if isinstance(c, int) and c == CHUNKS - 1 and slot > MLP_SLOT else 0

        def slot_count(c, slot):
            return c * SLOTS + slot + 2 - missing(c, slot)

        def before_in_acc(c, slot):
            return slot_count(c, slot - ACC_RING) if slot >= ACC_RING else slot_count(c - 1, slot - ACC_RING + SLOTS)

        def split_count(c, slot):
            return c * SPLITS + split_of(slot) + 2 - missing(c, slot)

        def acc_slot(slot):
            return acc[:, slot % ACC_RING, 0:CHUNK]

        def out_tile(layer, m):
            if layer == 1:
                return h_b, m
            return h_a, m + (4 if layer == 3 else 0)

        def in_tile(layer, k, part):
            kk = K_LAST if layer == 0 and k == 3 else P
            src = x0 if layer == 0 else h_b if layer == 2 else h_a
            return src[0:kk, k, part, :]

        def weight(part, layer, m, k):
            kk = K_LAST if layer == 0 and k == 3 else P
            t = TILE0[layer] + m * K_TILES[layer] + k
            return part[0:kk, t * P:(t + 1) * P]

        def out_count(c):
            return slot_count(c + 1, OUT_SLOT) - (2 if isinstance(c, int) and c == CHUNKS - 1 else 0)

        def weight_bank(n):
            if n < BETWEEN_UNITS:
                return acc[:, n % ACC_RING, :]
            return gram_ps[:, n % (GRAM_RING * GRAM_BANKS), :]

        def tile_of_group(g):
            return 4 * (g if g < W0_GROUPS else g - 1)

        def cols(ap):
            return ap.rearrange("p (s i) -> p s i", s=GROUP)

        def by_sample(ap):
            return ap.rearrange("p (i s) -> p s i", s=GROUP)

        block = ctx.enter_context(nc.Block())

        @block.sync
        def _(sp):
            def load_rows(d, u):
                if not (isinstance(d, int) and d == 0 and u < ROWS_RING):
                    sp.wait_ge(turned, d * UNITS + u + 1 - ROWS_RING)
                r = u % ROWS_RING
                sp.dma_start(rows[0:GROUP_ROWS, r], x_view[d, u]).then_inc(rows_loaded[r], 16)

            def load_weights(dst, w, m0, m1, loaded):
                sp.dma_start(dst, w.rearrange("(m p) k -> p m k", p=P)[:, m0:m1]).then_inc(loaded, 16)

            def spill(d):
                if isinstance(d, int) and d == 0:
                    sp.wait_ge(pairs_zeroed, 1)
                sp.wait_ge(grams_done, d * UNITS + UNITS)
                for s in range(GROUP):
                    sp.dma_start(blocks[:, :, s * RUN:(s + 1) * RUN],
                                 grams[QUAD * s:QUAD * s + FEATS, :, :]).then_inc(spilled, 16)

            def gather(d):
                sp.wait_ge(spilled, (d + 1) * GROUP * 16)
                for f, nf, k, nk, q in PIECES:
                    src = bass.AP(flat_blocks.tensor, ((FEATS + 1) * f + k) * CHUNK,
                                  [[(FEATS + 1) * CHUNK, nf], [CHUNK, nk], [1, CHUNK]])
                    sp.dma_start(pairs[q % P:q % P + nf * nk, q // P], src).then_inc(gathered, 16)

            def load_mlp(d):
                sp.dma_start(mlp_rows[:, :, :], mlp_view[d]).then_inc(mlp_loaded, 16)

            def store_y(c):
                sp.wait_ge(drained, out_count(c))
                sp.dma_start(y_view[c], y_row[:, :]).then_inc(y_stored, 16)

            def chunk(c):
                sp.wait_ge(filled, 1 if isinstance(c, int) and c == 0 else slot_count(c - 1, MLP_SLOT))
                load_mlp(c + 1)
                for u in range(ROWS_RING, UNITS):
                    load_rows(c + 1, u)
                    if u == 7 and not (isinstance(c, int) and c == 0):
                        store_y(c - 1)
                spill(c + 1)
                gather(c + 1)
                if not (isinstance(c, int) and c == CHUNKS - 2):
                    for u in range(ROWS_RING):
                        load_rows(c + 2, u)

            load_rows(0, 0)
            load_rows(0, 1)
            load_weights(stage_w0[:, 0:4, :], w0, 0, 4, w0_loaded[0])
            for u in range(2, 6):
                load_rows(0, u)
            load_weights(stage_b[:, :, :], w1, 0, 4, w1_head_loaded)
            for u in range(6, 10):
                load_rows(0, u)
            load_weights(stage_w0[:, 4:8, :], w0, 4, 8, w0_loaded[1])
            load_rows(0, 10)
            load_weights(stage_w3[:, :, :], w3, 0, 2, w3_loaded)
            load_rows(0, 11)
            load_mlp(0)
            load_rows(0, 12)
            r = 0
            for b, m in zip(biases + [w_out], M_TILES + [2]):
                src = b.rearrange("o (m p) -> (o m) p", p=P) if b is w_out else b.rearrange("(m p) -> m p", p=P)
                sp.dma_start(stage_small[r:r + m, :], src).then_inc(small_loaded, 16)
                r += m
            sp.dma_start(bout[:, :], b_out.rearrange("(o n) -> o n", o=1)).then_inc(small_loaded, 16)
            for u in range(13, UNITS):
                load_rows(0, u)
            sp.wait_ge(w_turned, ORDER.index(W1_HEAD[-1]) + 1)
            load_weights(stage_b[:, :, :], w2, 0, 4, w2_loaded)
            spill(0)
            sp.wait_ge(w_turned, ORDER.index(W0_ALL[-1]) + 1)
            load_weights(stage_a[:, :, :], w1, 4, 8, w1_tail_loaded)
            gather(0)
            for u in range(ROWS_RING):
                load_rows(1, u)
            chunk(0)
            with sp.Fori(1, CHUNKS - 2) as c:
                chunk(c)
            chunk(CHUNKS - 2)
            store_y(CHUNKS - 2)
            store_y(CHUNKS - 1)
            sp.wait_ge(y_stored, 16 * CHUNKS)

        @block.gpsimd
        def _(pool):
            nc.gpsimd.memset(ident[:], 0.0).then_inc(ident_ready, 1)
            pool.wait_ge(ident_ready, 1)
            nc.gpsimd.affine_select(out=ident[:], in_=ident[:], compare_op=ALU.not_equal, fill=1.0, base=0,
                                    pattern=[[-1, P]], channel_multiplier=1).then_inc(ident_ready, 1)
            nc.gpsimd.memset(pairs[:], 0.0).then_inc(pairs_zeroed, 1)

            for i in range(2):
                pool.wait_ge(w0_loaded[i], 16)
                if i == 1:
                    pool.wait_ge(w_turned, ORDER.index(3) + 1)
                rows_of = stage_w0[:, 4 * i:4 * i + 4, DIM:]
                for col, n, q, step in ROW_RUNS:
                    nc.gpsimd.tensor_copy(w0_ordered[:, :, q:q + (n - 1) * step + 1:step], rows_of[:, :, col:col + n])
                nc.gpsimd.tensor_copy(w0_ordered[:, :, PAIRS:], rows_of[:, :, PAIRS:]).then_inc(w0_in_order, 1)

        @block.tensor
        def _(pe):
            def turn_weights(n):
                g, bank = ORDER[n], weight_bank(n)
                ring = ACC_RING if n < BETWEEN_UNITS else GRAM_RING * GRAM_BANKS
                if n - ring >= (0 if n < BETWEEN_UNITS else BETWEEN_UNITS):
                    pe.wait_ge(w_done, n + 1 - ring)
                elif n >= BETWEEN_UNITS:
                    pe.wait_ge(parts_done, UNITS)
                if g < W0_GROUPS:
                    if g % 4 == 0:
                        pe.wait_ge(w0_in_order, g // 4 + 1)
                    for k in range(4):
                        kk = K_LAST if k == 3 else P
                        src = w0_ordered[:, g % 4, (k - 1) * P:(k - 1) * P + kk] if k else stage_w0[:, g, 0:P]
                        last = nc.tensor.transpose(bank[0:kk, k * P:(k + 1) * P], src, ident[:])
                elif g == W0_GROUPS:
                    pe.wait_ge(small_loaded, 6 * 16)
                    last = nc.tensor.transpose(bank[:, 0:24], stage_small[0:24, :], ident[0:24, 0:24])
                else:
                    m, part = (g - W0_GROUPS - 1) // 2, (g - W0_GROUPS - 1) % 2
                    src, loaded = [(stage_b[:, m % 4], w1_head_loaded), (stage_a[:, m % 4], w1_tail_loaded),
                                   (stage_b[:, m % 4], w2_loaded),
                                   (stage_w3.rearrange("p m k -> p (m k)"), w3_loaded)][m // 4]
                    if m % 4 == 0 and part == 0:
                        pe.wait_ge(loaded, 16)
                    for k in range(4):
                        at = (4 * part + k) * P
                        last = nc.tensor.transpose(bank[:, k * P:(k + 1) * P], src[:, at:at + P], ident[:])
                last.then_inc(w_turned, 1)

            def turn(d, u):
                r = u % ROWS_RING
                pe.wait_ge(rows_loaded[r], (d * (UNITS // ROWS_RING) + u // ROWS_RING + 1) * 16)
                if not (isinstance(d, int) and d == 0 and u < TURN_RING):
                    pe.wait_ge(xt_done, d * UNITS + u + 1 - TURN_RING)
                for j in range(UNIT_GROUPS):
                    last = nc.tensor.transpose(turned_ps[:, u % TURN_RING, j * GROUP_ROWS:(j + 1) * GROUP_ROWS],
                                               rows[0:GROUP_ROWS, r, j, :],
                                               ident[0:GROUP_ROWS, 0:GROUP_ROWS])
                last.then_inc(turned, 1)

            def gram(d, u):
                pe.wait_ge(xt_done, d * UNITS + u + 1)
                if not (isinstance(d, int) and d == 0 and u < GRAM_RING):
                    pe.wait_ge(parts_done, d * UNITS + u + 1 - GRAM_RING)
                for j in range(UNIT_GROUPS):
                    at = j % 2 * 2 * P
                    last = nc.tensor.matmul(gram_ps[:, u % GRAM_RING * GRAM_BANKS + j // 2, at:at + 2 * P], xt[:, u % XT_RING, j, 0, :],
                                            xt[:, u % XT_RING, j].rearrange("p h n -> p (h n)"), start=True, stop=True)
                last.then_inc(gram_done, 1)

            def turn_mlp(slot):
                for t in range(2):
                    last = nc.tensor.transpose(acc_slot(slot)[:, t * P:(t + 1) * P], mlp_rows[:, t, :], ident[:])
                return last

            def products(c, layer, m, k0, k1):
                slot = slot_of(layer, m)
                if k0 == 0:
                    if isinstance(c, int) and c == 0 and slot < ACC_RING - 1:
                        pe.wait_ge(w_done, W_GROUPS)
                    else:
                        pe.wait_ge(drained, before_in_acc(c, slot))
                if layer == 0 and m == 0:
                    if k0 == 0:
                        pe.wait_ge(pairs_done, c + 1)
                        pe.wait_ge(split_done, 1 if isinstance(c, int) and c == 0 else split_count(c - 1, MLP_SLOT))
                for k in range(k0, k1):
                    if layer > 0 and m == 0:
                        pe.wait_ge(split_done, split_count(c, slot_of(layer - 1, k)))
                    for n, (wp, xp) in enumerate(((w_hi, 0), (w_hi, 1), (w_lo, 0))):
                        last = nc.tensor.matmul(acc_slot(slot), weight(wp, layer, m, k), in_tile(layer, k, xp),
                                                start=(k == 0 and n == 0), stop=(k == K_TILES[layer] - 1 and n == 2))
                if k1 == K_TILES[layer]:
                    last.then_inc(filled, 2 if isinstance(c, int) and c == 0 and slot == 0 else 1)

            def out_row(c):
                pe.wait_ge(split_done, split_count(c, slot_of(3, 1)))
                pe.wait_ge(drained, before_in_acc(c + 1, OUT_SLOT))
                for k in range(2):
                    for n, (wp, xp) in enumerate(((wout_hi, 0), (wout_hi, 1), (wout_lo, 0))):
                        last = nc.tensor.matmul(acc_slot(OUT_SLOT)[0:1], wp[:, k:k + 1], h_a[:, 4 + k, xp, :],
                                                start=(k == 0 and n == 0), stop=(k == 1 and n == 2))
                last.then_inc(filled, 1)

            def chunk(c):
                ends = isinstance(c, int) and c == CHUNKS - 1
                for step in chunk_steps(not ends):
                    if step[0] == "mm":
                        products(c, *step[1:])
                    elif step[0] == "turn":
                        turn(c + 1, step[1])
                    elif step[0] == "gram":
                        gram(c + 1, step[1])
                    elif step[0] == "out" and not (isinstance(c, int) and c == 0):
                        out_row(c - 1)
                    elif step[0] == "mlp":
                        pe.wait_ge(mlp_loaded, (c + 2) * 16)
                        pe.wait_ge(drained, before_in_acc(c, MLP_SLOT))
                        turn_mlp(MLP_SLOT).then_inc(filled, 1)

            pe.wait_ge(ident_ready, 2)
            for u in range(UNITS + XT_LAG):
                if u < UNITS:
                    turn(0, u)
                if u >= XT_LAG:
                    gram(0, u - XT_LAG)
                if 0 <= u - FIRST_BETWEEN < BETWEEN_UNITS:
                    turn_weights(u - FIRST_BETWEEN)
            for n in range(BETWEEN_UNITS, W_GROUPS):
                turn_weights(n)
            pe.wait_ge(w_done, W_GROUPS)
            pe.wait_ge(mlp_loaded, 16)
            turn_mlp(SLOTS - 1).then_inc(filled, 1)
            chunk(0)
            with pe.Fori(1, CHUNKS - 1) as c:
                chunk(c)
            chunk(CHUNKS - 1)
            out_row(CHUNKS - 1)

        @block.scalar
        def _(act):
            def weights_hi(n):
                g, bank = ORDER[n], weight_bank(n)
                act.wait_ge(w_turned, n + 1)
                t = tile_of_group(g)
                if g == W0_GROUPS:
                    nc.scalar.activation(small_t[:], bank[:, 0:24], ACT.Copy)
                    last = nc.scalar.activation(wout_hi[:], bank[:, 22:24], ACT.Copy)
                elif g < W0_GROUPS:
                    nc.scalar.activation(w_hi[:, t * P:(t + 3) * P], bank[:, 0:3 * P], ACT.Copy)
                    last = nc.scalar.activation(w_hi[0:K_LAST, (t + 3) * P:(t + 4) * P],
                                                bank[0:K_LAST, 3 * P:4 * P], ACT.Copy)
                else:
                    last = nc.scalar.activation(w_hi[:, t * P:(t + 4) * P], bank, ACT.Copy)
                last.then_inc(w_hi_done, 1)

            def turned_hi(d, u):
                act.wait_ge(turned, d * UNITS + u + 1)
                if isinstance(d, int) and d == 0 and u < XT_RING:
                    act.wait_ge(xt_zeroed, 1)
                else:
                    act.wait_ge(gram_done, d * UNITS + u + 1 - XT_RING)
                nc.scalar.activation(
                    xt[:, u % XT_RING, :, 0, :].rearrange("p j (s f) -> p j s f", s=GROUP)[:, :, :, 0:FEATS],
                    turned_ps[:, u % TURN_RING, 0:UNIT_COLS].rearrange("p (j s f) -> p j s f", s=GROUP, f=FEATS),
                    ACT.Copy).then_inc(xt_hi_done, 1)

            def gram_parts(d, u):
                act.wait_ge(gram_done, d * UNITS + u + 1)
                if not (isinstance(d, int) and d == 0 and u < 2):
                    act.wait_ge(grams_done, d * UNITS + u - 1)
                else:
                    act.wait_ge(parts_zeroed, 1)
                b = u % GRAM_RING * GRAM_BANKS
                for s in range(GROUP):
                    quad = slice(QUAD * s, QUAD * s + FEATS)
                    last = nc.scalar.activation(
                        parts[quad, u % 2, :, :, 0:FEATS],
                        gram_ps[quad, b:b + GRAM_BANKS, :].rearrange("p a (b h n) -> p h (a b) n", h=2, n=P)[
                            :, :, :, QUAD * s:QUAD * s + FEATS], ACT.Copy)
                last.then_inc(parts_done, 1)

            def drain(c, slot, full, src, func, **kw):
                act.wait_ge(filled, slot_count(c, slot))
                if slot == 2 or slot > 3:
                    act.wait_ge(split_done, split_count(c, slot - 2))
                elif slot == 3 and isinstance(c, int) and c == 0:
                    act.wait_ge(split_done, 1)
                elif not (isinstance(c, int) and c == 0):
                    act.wait_ge(split_done, split_count(c - 1, SLOTS - 2 if slot == 0 else SLOTS - 1))
                nc.scalar.activation(full, src, func, **kw).then_inc(
                    drained, 2 if isinstance(c, int) and c == 0 and slot == 0 else 1)

            def pairs_hi(d):
                act.wait_ge(gathered, (d + 1) * 16 * len(PIECES))
                nc.scalar.activation(x0[:, 1:4, 0, :], pairs[:], ACT.Copy).then_inc(pairs_hi_done, 1)

            def out_row(c):
                act.wait_ge(filled, out_count(c))
                if not (isinstance(c, int) and c == 0):
                    act.wait_ge(y_stored, c * 16)
                nc.scalar.activation(by_sample(y_row[:, :]), cols(acc_slot(OUT_SLOT)[0:1]), ACT.Identity,
                                     bias=bout[:, :]).then_inc(drained, 1)

            def chunk(c):
                ends = isinstance(c, int) and c == CHUNKS - 1
                for step in chunk_steps(not ends):
                    if step[0] == "mm":
                        _, layer, m, _, k1 = step
                        if k1 == K_TILES[layer]:
                            bias = small_t[:, sum(M_TILES[:layer]) + m:sum(M_TILES[:layer]) + m + 1]
                            slot = slot_of(layer, m)
                            drain(c, slot, h_full[:, slot % 2, :], acc_slot(slot), ACT.Relu, bias=bias)
                    elif step[0] == "turn":
                        turned_hi(c + 1, step[1])
                    elif step[0] == "gram":
                        gram_parts(c + 1, step[1])
                    elif step[0] == "mlp":
                        drain(c, MLP_SLOT, cols(h_full[:, MLP_SLOT % 2, :]), by_sample(acc_slot(MLP_SLOT)), ACT.Copy)
                    elif step[0] == "pairs":
                        pairs_hi(c + 1)
                    elif step[0] == "out" and not (isinstance(c, int) and c == 0):
                        out_row(c - 1)

            for u in range(UNITS + XT_LAG):
                if u < UNITS:
                    turned_hi(0, u)
                if u >= XT_LAG:
                    gram_parts(0, u - XT_LAG)
                if 0 <= u - FIRST_BETWEEN < BETWEEN_UNITS:
                    weights_hi(u - FIRST_BETWEEN)
            for n in range(BETWEEN_UNITS, W_GROUPS):
                weights_hi(n)
            act.wait_ge(filled, 1)
            nc.scalar.activation(cols(h_full[:, 1, :]), by_sample(acc_slot(SLOTS - 1)), ACT.Copy).then_inc(drained, 1)
            pairs_hi(0)
            chunk(0)
            with act.Fori(1, CHUNKS - 1) as c:
                chunk(c)
            chunk(CHUNKS - 1)
            out_row(CHUNKS - 1)

        @block.vector
        def _(dve):
            def weights_lo(n):
                g, bank = ORDER[n], weight_bank(n)
                dve.wait_ge(w_hi_done, n + 1)
                t = tile_of_group(g)
                if g == W0_GROUPS:
                    last = nc.vector.tensor_tensor(wout_lo[:], bank[:, 22:24], wout_hi[:].bitcast(F32), ALU.subtract)
                elif g < W0_GROUPS:
                    a, b = t * P, (t + 3) * P
                    nc.vector.tensor_tensor(w_lo[:, a:b], bank[:, 0:3 * P], w_hi[:, a:b].bitcast(F32), ALU.subtract)
                    a, b = b, b + P
                    last = nc.vector.tensor_tensor(w_lo[0:K_LAST, a:b], bank[0:K_LAST, 3 * P:4 * P],
                                                   w_hi[0:K_LAST, a:b].bitcast(F32), ALU.subtract)
                else:
                    a, b = t * P, (t + 4) * P
                    last = nc.vector.tensor_tensor(w_lo[:, a:b], bank, w_hi[:, a:b].bitcast(F32), ALU.subtract)
                last.then_inc(w_done, 1)

            def turned_lo(d, u):
                dve.wait_ge(xt_hi_done, d * UNITS + u + 1)
                hi, lo = (xt[:, u % XT_RING, :, h, :].rearrange("p j (s f) -> p j s f", s=GROUP)[:, :, :, 0:FEATS]
                          for h in range(2))
                nc.vector.tensor_tensor(
                    lo, turned_ps[:, u % TURN_RING, 0:UNIT_COLS].rearrange("p (j s f) -> p j s f", s=GROUP, f=FEATS),
                    hi.bitcast(F32), ALU.subtract).then_inc(xt_done, 1)

            def gram_sum(d, u):
                n = d * UNITS + u + 1
                hh, hl = parts[:, u % 2, 0], parts[:, u % 2, 1]
                dve.wait_ge(parts_done, n)
                if not (isinstance(d, int) and d == 0 and u == 0):
                    dve.wait_ge(grams_done, n - 1)
                nc.vector.transpose(low_t[:, :, :].rearrange("p j g -> p (j g)"),
                                    hl.rearrange("p j g -> p (j g)")).then_inc(low_turned, 1)
                nc.vector.tensor_tensor(hh, hh, hl, ALU.add).then_inc(sum_done, 1)
                dve.wait_ge(low_turned, n)
                dve.wait_ge(sum_done, n)
                if not (isinstance(d, int) and d == 0) and u == 0:
                    dve.wait_ge(spilled, d * GROUP * 16)
                nc.vector.tensor_tensor(
                    grams[:, :, u * UNIT_GROUPS:(u + 1) * UNIT_GROUPS].rearrange("p g j -> p j g"),
                    hh[:, :, 0:FEATS], low_t[:, :, 0:FEATS], ALU.add).then_inc(grams_done, 1)

            def split(full, high, low, n):
                nc.vector.tensor_copy(high, full).then_inc(high_done, 1)
                dve.wait_ge(high_done, n)
                nc.vector.tensor_tensor(low, full, high.bitcast(F32), ALU.subtract).then_inc(split_done, 1)

            def split_slot(c, slot, h, t):
                dve.wait_ge(drained, slot_count(c, slot))
                split(h_full[:, slot % 2, :], h[:, t, 0, :], h[:, t, 1, :], split_count(c, slot))

            def pairs_lo(d):
                dve.wait_ge(pairs_hi_done, d + 1)
                nc.vector.tensor_tensor(x0[:, 1:4, 1, :], pairs[:], x0[:, 1:4, 0, :].bitcast(F32),
                                        ALU.subtract).then_inc(pairs_done, 1)

            def chunk(c):
                ends = isinstance(c, int) and c == CHUNKS - 1
                for step in chunk_steps(not ends):
                    if step[0] == "mm":
                        _, layer, m, _, k1 = step
                        if k1 == K_TILES[layer]:
                            split_slot(c, slot_of(layer, m), *out_tile(layer, m))
                    elif step[0] == "turn":
                        turned_lo(c + 1, step[1])
                    elif step[0] == "gram":
                        gram_sum(c + 1, step[1])
                    elif step[0] == "mlp":
                        split_slot(c, MLP_SLOT, x0, 0)
                    elif step[0] == "pairs":
                        pairs_lo(c + 1)

            nc.vector.memset(xt[:].bitcast(F32), 0.0).then_inc(xt_zeroed, 1)
            nc.vector.memset(parts[:], 0.0).then_inc(parts_zeroed, 1)
            for u in range(UNITS + XT_LAG):
                if u < UNITS:
                    turned_lo(0, u)
                if u >= XT_LAG:
                    gram_sum(0, u - XT_LAG)
                if 0 <= u - FIRST_BETWEEN < BETWEEN_UNITS:
                    weights_lo(u - FIRST_BETWEEN)
            for n in range(BETWEEN_UNITS, W_GROUPS):
                weights_lo(n)
            dve.wait_ge(drained, 1)
            split(h_full[:, 1, :], x0[:, 0, 0, :], x0[:, 0, 1, :], 1)
            pairs_lo(0)
            chunk(0)
            with dve.Fori(1, CHUNKS - 1) as c:
                chunk(c)
            chunk(CHUNKS - 1)


_INS = ['r_bottom_output', 'r_bottom_mlp_output', 'L0_rec_w0', 'L0_rec_b0', 'L0_rec_w1', 'L0_rec_b1', 'L0_rec_w2',
        'L0_rec_b2', 'L0_rec_w3', 'L0_rec_b3', 'L0_rec_w_out', 'L0_rec_b_out']
_OUTS = [((2048, 1), 'float32')]


def kernel(**inputs):
    import numpy as _np
    import concourse.bacc as _bacc
    from concourse import mybir as _mybir
    from concourse.bass_utils import run_bass_kernel_spmd as _run

    nc = _bacc.Bacc("TRN2", target_bir_lowering=False, num_devices=1, dynamic_dma_scratch_size=2048)
    arrays, args = {}, []
    for name in _INS:
        a = _np.ascontiguousarray(inputs[name])
        arrays[f"in_{name}_dram"] = a
        args.append(nc.dram_tensor(f"in_{name}_dram", a.shape, _mybir.dt.from_np(a.dtype), kind="ExternalInput").ap())
    for i, (shape, dtype) in enumerate(_OUTS):
        dt = _mybir.dt.from_np(_np.dtype(dtype))
        args.append(nc.dram_tensor(f"out_{i}_dram", shape, dt, kind="ExternalOutput").ap())
    dlrm_program(nc, *args)
    r = _run(nc, [arrays], core_ids=[0])
    return r.results[0]["out_0_dram"]
```

```python
from contextlib import ExitStack

import concourse.bass as bass
from concourse import mybir

F32 = mybir.dt.float32
F32R = mybir.dt.float32r
ALU = mybir.AluOpType
ACT = mybir.ActivationFunctionType

BATCH, FEATS, DIM = 2048, 27, 128
PAIRS = FEATS * (FEATS - 1) // 2
LAYERS = [(DIM + PAIRS + 1, 1024), (1024, 1024), (1024, 512), (512, 256)]
P = 128

CHUNK = 256
CHUNKS = BATCH // CHUNK
GROUP = 4
RUN = CHUNK // GROUP
GROUP_ROWS = GROUP * FEATS
QUAD = 32
UNIT_GROUPS = 4
UNIT_COLS = UNIT_GROUPS * GROUP_ROWS
UNITS = RUN // UNIT_GROUPS
ROWS_RING = 4

K_TILES = [-(-k // P) for k, _ in LAYERS]
M_TILES = [m // P for _, m in LAYERS]
TILE0 = [sum(K_TILES[j] * M_TILES[j] for j in range(n)) for n in range(5)]
K_LAST = LAYERS[0][0] - 3 * P
W0_GROUPS = TILE0[1] // 4
W_GROUPS = TILE0[4] // 4 + 1
W1_HEAD, W0_ALL, SMALL = list(range(9, 17)), list(range(W0_GROUPS)), [W0_GROUPS]
W1_TAIL, W2_ALL, W3_ALL = list(range(17, 25)), list(range(25, 33)), list(range(33, 35))
ORDER = W1_HEAD + W0_ALL + SMALL + W3_ALL + W2_ALL + W1_TAIL
BETWEEN_UNITS, FIRST_BETWEEN = 8, 7
BEFORE_CHUNK = W_GROUPS - len(W1_TAIL)
W0_TURNED = ORDER.index(W0_ALL[-1]) + 1
assert W0_TURNED >= BETWEEN_UNITS

FIRST_SLOT = [sum(M_TILES[:n]) for n in range(4)]
SLOTS = sum(M_TILES)
LAST_LAYER = [(0, 0, 3), (1, 0, 2), (0, 3, 4), (1, 2, 4)]

ACC_RING, TURN_RING, GRAM_RING = 2, 2, 2
GRAM_BANKS = 2
XT_RING, XT_LAG = 4, 2
assert ACC_RING + TURN_RING + GRAM_RING * GRAM_BANKS == 8 and SLOTS % ACC_RING == 0

HOOK = 9
OUT_UNIT = 2


def slot_of(layer, m):
    return FIRST_SLOT[layer] + m


BAND = [14 if f < 13 else 13 for f in range(FEATS - 1)]
BAND0 = [sum(BAND[:f]) for f in range(FEATS)]
assert BAND0[-1] == PAIRS


def band_pieces():
    out, q = [], 0
    while q < PAIRS:
        f = max(f for f in range(FEATS - 1) if BAND0[f] <= q)
        room = P - q % P
        k, whole = q - BAND0[f] + 1, 1
        n = min(BAND[f] + 1 - k, room)
        if k == 1 and n == BAND[f]:
            while f + whole < FEATS - 1 and BAND[f + whole] == n and (whole + 1) * n <= room:
                whole += 1
        out.append((f, whole, k, n, q))
        q += whole * n
    return out


PIECES = band_pieces()


def band_of_rows():
    out = []
    for a in range(1, FEATS):
        place = []
        for b in range(a):
            flat = min(x for x in (b * FEATS + a, a * FEATS + b) if 1 <= x % (FEATS + 1) <= BAND[x // (FEATS + 1)])
            place.append(BAND0[flat // (FEATS + 1)] + flat % (FEATS + 1) - 1)
        b = 0
        while b < a:
            n = 1
            while b + n < a and place[b + n] - place[b + n - 1] == (place[b + 1] - place[b]) > 0:
                n += 1
            out.append((a * (a - 1) // 2 + b, n, place[b], place[b + 1] - place[b] if n > 1 else 1))
            b += n
    return out


ROW_RUNS = band_of_rows()
assert sorted(q + i * d for _, n, q, d in ROW_RUNS for i in range(n)) == list(range(PAIRS))

def unit_steps(n):
    steps, g = [], n - XT_LAG
    if n < UNITS:
        steps.append(("turn", n))
    if g >= 1:
        steps.append(("sum", g - 1))
    if g >= 0:
        steps.append(("gram", g))
    if g == UNITS - 1:
        steps.append(("sum", g))
    return steps


def first_steps():
    steps = []
    for u in range(UNITS + XT_LAG):
        steps += unit_steps(u)
        if 0 <= u - FIRST_BETWEEN < BETWEEN_UNITS:
            steps.append(("weights", u - FIRST_BETWEEN))
    steps += [("weights", n) for n in range(BETWEEN_UNITS, W0_TURNED)] + [("mlp",)]
    return steps + [("weights", n) for n in range(W0_TURNED, BEFORE_CHUNK)] + [("pairs",)]


def chunk_steps(gram, weights=False):
    steps, done, unit, group = [], 0, 0, BEFORE_CHUNK if weights else W_GROUPS

    def hook():
        nonlocal unit, group
        if group < W_GROUPS:
            steps.append(("weights", group))
            group += 1
        elif gram and unit < UNITS + XT_LAG:
            steps.extend(unit_steps(unit))
            unit += 1

    for layer in range(3):
        for m in range(M_TILES[layer]):
            if (layer, m) == (2, 2) and gram:
                steps.append(("mlp",))
            k = 0
            while k < K_TILES[layer]:
                n = K_TILES[layer] - k
                if layer < 2:
                    n = min(n, (HOOK - done % HOOK) // 3)
                steps.append(("mm", layer, m, k, k + n))
                k += n
                done += 3 * n
                if layer < 2 and done % HOOK == 0:
                    hook()
                if done == OUT_UNIT * HOOK:
                    steps.append(("out",))
    if gram:
        steps.append(("pairs",))
    steps += [("mm", 3, m, k0, k1) for m, k0, k1 in LAST_LAYER]
    return steps


def dlrm_program(nc, x, x_mlp, w0, b0, w1, b1, w2, b2, w3, b3, w_out, b_out, y):
    weights = [w0, w1, w2, w3]
    biases = [b0, b1, b2, b3]
    with ExitStack() as ctx:
        def sb(name, shape, dt=F32):
            return ctx.enter_context(nc.sbuf_tensor(name, shape, dt))

        def sem(name):
            return ctx.enter_context(nc.semaphore(name))

        def shared(*specs):
            with ExitStack() as inner:
                return [inner.enter_context(nc.sbuf_tensor(n, s, F32)) for n, s in specs]

        w_hi = sb("w_hi", [P, TILE0[4] * P], F32R)
        w_lo = sb("w_lo", [P, TILE0[4] * P], F32R)
        w0_ordered, = shared(("w0_ordered", [P, 8, PAIRS + 1]))
        x0 = sb("x0", [P, 4, 2, CHUNK], F32R)
        pairs = sb("pairs", [P, 3, CHUNK])
        h_full = sb("h_full", [P, 2, CHUNK])
        stage_pairs, _, stage_dense = shared(("stage_pairs", [P, 8, PAIRS + 1]),
                                             ("stage_gap", [P, 3 * 1024 - 8 * (PAIRS + 1)]),
                                             ("stage_dense", [P, 8, DIM]))
        stage_a, = shared(("stage_a", [P, 4, 1024]))
        h_a = sb("h_a", [P, 8, 2, CHUNK], F32R)
        stage_b, = shared(("stage_b", [P, 4, 1024]))
        h_b = sb("h_b", [P, 8, 2, CHUNK], F32R)
        stage_w3 = sb("stage_w3", [P, 2, 512])
        rows = sb("rows", [P, ROWS_RING, UNIT_GROUPS, DIM])
        mlp_rows = sb("mlp_rows", [P, 2, P])
        xt = sb("xt", [P, XT_RING, UNIT_GROUPS, 2, GROUP * QUAD], F32R)
        parts = sb("parts", [P, 2, 2, UNIT_GROUPS, QUAD])
        low_t = sb("low_t", [P, 2, UNIT_GROUPS, QUAD])
        grams = sb("grams", [P, FEATS, RUN])
        ident = sb("ident", [P, P])
        stage_small, = shared(("stage_small", [24, P]))
        y_row = sb("y_row", [1, CHUNK])
        small_t = sb("small_t", [P, 24])
        ones = sb("ones", [P, 1], F32R)
        bout = sb("bout", [1, 1])

        acc = ctx.enter_context(nc.psum_tensor("acc", [P, ACC_RING, 512], F32))
        turned_ps = ctx.enter_context(nc.psum_tensor("turned_ps", [P, TURN_RING, 512], F32))
        gram_ps = ctx.enter_context(nc.psum_tensor("gram_ps", [P, GRAM_RING * GRAM_BANKS, 512], F32))

        small_loaded = sem("small_loaded")
        w0_loaded = sem("w0_loaded")
        w0_in_order = sem("w0_in_order")
        w0_dense_loaded = sem("w0_dense_loaded")
        w1_head_loaded = [sem(f"w1_head_loaded{i}") for i in range(2)]
        w1_tail_loaded = sem("w1_tail_loaded")
        w2_loaded = [sem(f"w2_loaded{i}") for i in range(2)]
        w3_loaded = sem("w3_loaded")
        rows_loaded = [sem(f"rows_loaded{i}") for i in range(ROWS_RING)]
        mlp_loaded = sem("mlp_loaded")
        ident_ready = sem("ident_ready")
        pairs_zeroed = sem("pairs_zeroed")
        xt_zeroed = sem("xt_zeroed")
        parts_zeroed = sem("parts_zeroed")
        w_turned = sem("w_turned")
        w_hi_done = sem("w_hi_done")
        w_done = sem("w_done")
        turned = sem("turned")
        xt_hi_done = sem("xt_hi_done")
        xt_done = sem("xt_done")
        gram_done = sem("gram_done")
        parts_done = sem("parts_done")
        low_turned = sem("low_turned")
        sum_done = sem("sum_done")
        grams_done = sem("grams_done")
        spilled = sem("spilled")
        gathered = sem("gathered")
        pairs_hi_done = sem("pairs_hi_done")
        pairs_done = sem("pairs_done")
        filled = sem("filled")
        drained = sem("drained")
        high_done = sem("high_done")
        split_done = sem("split_done")
        mlp_turned = sem("mlp_turned")
        mlp_hi_done = sem("mlp_hi_done")
        mlp_done = sem("mlp_done")
        summed_hi_done = sem("summed_hi_done")
        summed_done = sem("summed_done")
        out_filled = sem("out_filled")
        out_drained = sem("out_drained")
        y_stored = sem("y_stored")

        x_view = x.rearrange("(c u j s) f d -> c u (s f) j d", u=UNITS, j=UNIT_GROUPS, s=GROUP)
        mlp_view = x_mlp.rearrange("(c t p) d -> c p t d", t=2, p=P)
        y_view = y.rearrange("(c n) o -> c o n", n=CHUNK)
        blocks = nc.dram_tensor("blocks", (FEATS, FEATS, CHUNK), F32).ap()
        flat_blocks = blocks.rearrange("f g n -> (f g) n")

        def slot_count(c, slot):
            return c * SLOTS + slot + 1

        def acc_slot(slot):
            return acc[:, slot % ACC_RING, 0:CHUNK]

        mlp_bank = turned_ps[:, 0, 0:CHUNK]
        out_bank = turned_ps[0:1, OUT_UNIT % TURN_RING, 0:CHUNK]

        def in_tile(layer, k, part):
            kk = K_LAST if layer == 0 and k == 3 else P
            src = x0 if layer == 0 else h_b if layer == 2 else h_a
            return src[0:kk, k, part, :]

        def weight(part, layer, m, k):
            kk = K_LAST if layer == 0 and k == 3 else P
            t = TILE0[layer] + m * K_TILES[layer] + k
            return part[0:kk, t * P:(t + 1) * P]

        def weight_bank(n):
            if n < BETWEEN_UNITS:
                return acc[:, n % ACC_RING, :]
            return gram_ps[:, n % (GRAM_RING * GRAM_BANKS), :]

        def tile_of_group(g):
            return 4 * (g if g < W0_GROUPS else g - 1)

        def cols(ap):
            return ap.rearrange("p (s i) -> p s i", s=GROUP)

        def by_sample(ap):
            return ap.rearrange("p (i s) -> p s i", s=GROUP)

        block = ctx.enter_context(nc.Block())

        @block.sync
        def _(sp):
            def load_rows(d, u):
                if not (isinstance(d, int) and d == 0 and u < ROWS_RING):
                    sp.wait_ge(turned, d * UNITS + u + 1 - ROWS_RING)
                r = u % ROWS_RING
                sp.dma_start(rows[0:GROUP_ROWS, r], x_view[d, u]).then_inc(rows_loaded[r], 16)

            def load_weights(dst, w, m0, m1, loaded, k0=0, k1=None):
                sp.dma_start(dst, w.rearrange("(m p) k -> p m k", p=P)[:, m0:m1, k0:k1]).then_inc(loaded, 16)

            def spill(d):
                sp.wait_ge(grams_done, d * UNITS + UNITS)
                for s in range(GROUP):
                    sp.dma_start(blocks[:, :, s * RUN:(s + 1) * RUN],
                                 grams[QUAD * s:QUAD * s + FEATS, :, :]).then_inc(spilled, 16)

            def gather(d):
                sp.wait_ge(spilled, (d + 1) * GROUP * 16)
                if isinstance(d, int) and d == 0:
                    sp.wait_ge(pairs_zeroed, 1)
                for f, nf, k, nk, q in PIECES:
                    src = bass.AP(flat_blocks.tensor, ((FEATS + 1) * f + k) * CHUNK,
                                  [[(FEATS + 1) * CHUNK, nf], [CHUNK, nk], [1, CHUNK]])
                    sp.dma_start(pairs[q % P:q % P + nf * nk, q // P], src).then_inc(gathered, 16)

            def load_mlp(d):
                sp.dma_start(mlp_rows[:, :, :], mlp_view[d]).then_inc(mlp_loaded, 16)

            def store_y(c):
                sp.wait_ge(out_drained, c + 1)
                sp.dma_start(y_view[c], y_row[:, :]).then_inc(y_stored, 16)

            def chunk(c):
                sp.wait_ge(mlp_turned, c + 1)
                load_mlp(c + 1)
                for u in range(ROWS_RING, UNITS):
                    load_rows(c + 1, u)
                    if u == 7 and not (isinstance(c, int) and c == 0):
                        store_y(c - 1)
                spill(c + 1)
                gather(c + 1)
                if not (isinstance(c, int) and c == CHUNKS - 2):
                    for u in range(ROWS_RING):
                        load_rows(c + 2, u)

            for u in range(ROWS_RING):
                load_rows(0, u)
            load_weights(stage_pairs[:, :, :], w0, 0, 8, w0_loaded, k0=DIM)
            for u in range(ROWS_RING, 8):
                load_rows(0, u)
            load_weights(stage_b[:, 0:2, :], w1, 0, 2, w1_head_loaded[0])
            for u in range(8, 10):
                load_rows(0, u)
            load_weights(stage_b[:, 2:4, :], w1, 2, 4, w1_head_loaded[1])
            load_rows(0, 10)
            load_mlp(0)
            load_rows(0, 11)
            load_weights(stage_dense[:, :, :], w0, 0, 8, w0_dense_loaded, k1=DIM)
            load_rows(0, 12)
            r = 0
            for b, m in zip(biases + [w_out], M_TILES + [2]):
                src = b.rearrange("o (m p) -> (o m) p", p=P) if b is w_out else b.rearrange("(m p) -> m p", p=P)
                sp.dma_start(stage_small[r:r + m, :], src).then_inc(small_loaded, 16)
                r += m
            sp.dma_start(bout[:, :], b_out.rearrange("(o n) -> o n", o=1)).then_inc(small_loaded, 16)
            load_rows(0, 13)
            load_weights(stage_w3[:, :, :], w3, 0, 2, w3_loaded)
            for u in range(14, UNITS):
                load_rows(0, u)
            sp.wait_ge(w0_in_order, 1)
            load_weights(stage_a[:, 0:3, :], w2, 0, 3, w2_loaded[0])
            sp.wait_ge(w_turned, ORDER.index(W1_HEAD[-1]) + 1)
            load_weights(stage_b[:, :, :], w1, 4, 8, w1_tail_loaded)
            spill(0)
            sp.wait_ge(w_turned, W0_TURNED)
            load_weights(stage_a[:, 3:4, :], w2, 3, 4, w2_loaded[1])
            gather(0)
            for u in range(ROWS_RING):
                load_rows(1, u)
            chunk(0)
            with sp.Fori(1, CHUNKS - 2) as c:
                chunk(c)
            chunk(CHUNKS - 2)
            store_y(CHUNKS - 2)
            store_y(CHUNKS - 1)
            sp.wait_ge(y_stored, 16 * CHUNKS)

        @block.gpsimd
        def _(pool):
            nc.gpsimd.memset(ident[:], 0.0).then_inc(ident_ready, 1)
            pool.wait_ge(ident_ready, 1)
            nc.gpsimd.affine_select(out=ident[:], in_=ident[:], compare_op=ALU.not_equal, fill=1.0, base=0,
                                    pattern=[[-1, P]], channel_multiplier=1).then_inc(ident_ready, 1)
            pool.wait_ge(w0_loaded, 16)
            for col, n, q, step in ROW_RUNS:
                nc.gpsimd.tensor_copy(w0_ordered[:, :, q:q + (n - 1) * step + 1:step], stage_pairs[:, :, col:col + n])
            nc.gpsimd.tensor_copy(w0_ordered[:, :, PAIRS:], stage_pairs[:, :, PAIRS:]).then_inc(w0_in_order, 1)
            pool.wait_ge(w_turned, W0_TURNED)
            nc.gpsimd.memset(pairs[:], 0.0).then_inc(pairs_zeroed, 1)

        @block.tensor
        def _(pe):
            def turn_weights(n):
                g, bank = ORDER[n], weight_bank(n)
                ring = ACC_RING if n < BETWEEN_UNITS else GRAM_RING * GRAM_BANKS
                if n - ring >= (0 if n < BETWEEN_UNITS else BETWEEN_UNITS):
                    pe.wait_ge(w_done, n + 1 - ring)
                elif n >= BETWEEN_UNITS:
                    pe.wait_ge(parts_done, UNITS)
                if g < W0_GROUPS:
                    if g == 0:
                        pe.wait_ge(w0_in_order, 1)
                        pe.wait_ge(w0_dense_loaded, 16)
                    for k in range(4):
                        kk = K_LAST if k == 3 else P
                        src = w0_ordered[:, g, (k - 1) * P:(k - 1) * P + kk] if k else stage_dense[:, g, :]
                        last = nc.tensor.transpose(bank[0:kk, k * P:(k + 1) * P], src, ident[:])
                elif g == W0_GROUPS:
                    pe.wait_ge(small_loaded, 6 * 16)
                    last = nc.tensor.transpose(bank[:, 0:24], stage_small[0:24, :], ident[0:24, 0:24])
                else:
                    m, part = (g - W0_GROUPS - 1) // 2, (g - W0_GROUPS - 1) % 2
                    src, loaded = [(stage_b[:, m % 4], w1_head_loaded[m % 4 // 2]),
                                   (stage_b[:, m % 4], w1_tail_loaded),
                                   (stage_a[:, m % 4], w2_loaded[m % 4 // 3]),
                                   (stage_w3.rearrange("p m k -> p (m k)"), w3_loaded)][m // 4]
                    if part == 0:
                        pe.wait_ge(loaded, 16)
                    for k in range(4):
                        at = (4 * part + k) * P
                        last = nc.tensor.transpose(bank[:, k * P:(k + 1) * P], src[:, at:at + P], ident[:])
                last.then_inc(w_turned, 1)

            def turn(d, u):
                r = u % ROWS_RING
                pe.wait_ge(rows_loaded[r], (d * (UNITS // ROWS_RING) + u // ROWS_RING + 1) * 16)
                if not (isinstance(d, int) and d == 0 and u < TURN_RING):
                    pe.wait_ge(xt_done, d * UNITS + u + 1 - TURN_RING)
                if u == 0 and not (isinstance(d, int) and d == 0):
                    pe.wait_ge(mlp_done, d)
                if u == OUT_UNIT and not (isinstance(d, int) and d < 2):
                    pe.wait_ge(out_drained, d - 1)
                for j in range(UNIT_GROUPS):
                    last = nc.tensor.transpose(turned_ps[:, u % TURN_RING, j * GROUP_ROWS:(j + 1) * GROUP_ROWS],
                                               rows[0:GROUP_ROWS, r, j, :],
                                               ident[0:GROUP_ROWS, 0:GROUP_ROWS])
                last.then_inc(turned, 1)

            def gram(d, u):
                pe.wait_ge(xt_done, d * UNITS + u + 1)
                if isinstance(d, int) and d == 1 and u == 0:
                    pe.wait_ge(w_done, W_GROUPS)
                if not (isinstance(d, int) and d == 0 and u < GRAM_RING):
                    pe.wait_ge(parts_done, d * UNITS + u + 1 - GRAM_RING)
                for j in range(UNIT_GROUPS):
                    at = j % 2 * 2 * P
                    last = nc.tensor.matmul(gram_ps[:, u % GRAM_RING * GRAM_BANKS + j // 2, at:at + 2 * P],
                                            xt[:, u % XT_RING, j, 0, :],
                                            xt[:, u % XT_RING, j].rearrange("p h n -> p (h n)"), start=True, stop=True)
                last.then_inc(gram_done, 1)

            def turn_mlp(d):
                pe.wait_ge(mlp_loaded, (d + 1) * 16)
                pe.wait_ge(xt_done, (d + 1) * UNITS)
                for t in range(2):
                    last = nc.tensor.transpose(mlp_bank[:, t * P:(t + 1) * P], mlp_rows[:, t, :], ident[:])
                last.then_inc(mlp_turned, 1)

            def products(c, layer, m, k0, k1):
                slot = slot_of(layer, m)
                if k0 == 0:
                    if isinstance(c, int) and c == 0 and (layer, m) in ((0, 0), (1, 0), (1, 4)):
                        pe.wait_ge(w_done, {(0, 0): W0_TURNED, (1, 0): BEFORE_CHUNK, (1, 4): W_GROUPS}[layer, m])
                    if not (isinstance(c, int) and c == 0 and slot < ACC_RING):
                        pe.wait_ge(drained, slot_count(c, slot) - ACC_RING)
                for k in range(k0, k1):
                    if layer == 0 and m == 0:
                        if k == 0:
                            pe.wait_ge(mlp_done, c + 1)
                        else:
                            pe.wait_ge(pairs_done, c * 3 + k)
                    if layer > 0 and m == 0:
                        pe.wait_ge(split_done, slot_count(c, slot_of(layer - 1, k)))
                    for n, (wp, xp) in enumerate(((w_hi, 0), (w_hi, 1), (w_lo, 0))):
                        last = nc.tensor.matmul(acc_slot(slot), weight(wp, layer, m, k), in_tile(layer, k, xp),
                                                start=(k == 0 and n == 0), stop=(k == K_TILES[layer] - 1 and n == 2))
                if k1 == K_TILES[layer]:
                    last.then_inc(filled, 1)

            def out_row(c):
                last_units = isinstance(c, int) and c >= CHUNKS - 2
                pe.wait_ge(xt_done, CHUNKS * UNITS if last_units else (c + 2) * UNITS + OUT_UNIT - TURN_RING + 1)
                pe.wait_ge(summed_done, c + 1)
                for part in range(2):
                    last = nc.tensor.matmul(out_bank, ones[:], h_a[:, 4, part, :], start=(part == 0), stop=(part == 1))
                last.then_inc(out_filled, 1)

            def chunk(c):
                ends = isinstance(c, int) and c == CHUNKS - 1
                for step in chunk_steps(not ends, isinstance(c, int) and c == 0):
                    if step[0] == "mm":
                        products(c, *step[1:])
                    elif step[0] == "turn":
                        turn(c + 1, step[1])
                    elif step[0] == "gram":
                        gram(c + 1, step[1])
                    elif step[0] == "weights":
                        turn_weights(step[1])
                    elif step[0] == "out" and not (isinstance(c, int) and c == 0):
                        out_row(c - 1)
                    elif step[0] == "mlp":
                        turn_mlp(c + 1)

            pe.wait_ge(ident_ready, 2)
            for step in first_steps():
                if step[0] == "turn":
                    turn(0, step[1])
                elif step[0] == "gram":
                    gram(0, step[1])
                elif step[0] == "weights":
                    turn_weights(step[1])
                elif step[0] == "mlp":
                    turn_mlp(0)
            chunk(0)
            with pe.Fori(1, CHUNKS - 1) as c:
                chunk(c)
            chunk(CHUNKS - 1)
            out_row(CHUNKS - 1)

        @block.scalar
        def _(act):
            def weights_hi(n):
                g, bank = ORDER[n], weight_bank(n)
                act.wait_ge(w_turned, n + 1)
                t = tile_of_group(g)
                if g == W0_GROUPS:
                    last = nc.scalar.activation(small_t[:], bank[:, 0:24], ACT.Copy)
                elif g < W0_GROUPS:
                    nc.scalar.activation(w_hi[:, t * P:(t + 3) * P], bank[:, 0:3 * P], ACT.Copy)
                    last = nc.scalar.activation(w_hi[0:K_LAST, (t + 3) * P:(t + 4) * P],
                                                bank[0:K_LAST, 3 * P:4 * P], ACT.Copy)
                else:
                    last = nc.scalar.activation(w_hi[:, t * P:(t + 4) * P], bank, ACT.Copy)
                last.then_inc(w_hi_done, 1)

            def turned_hi(d, u):
                act.wait_ge(turned, d * UNITS + u + 1)
                if isinstance(d, int) and d == 0 and u < XT_RING:
                    act.wait_ge(xt_zeroed, 1)
                else:
                    act.wait_ge(gram_done, d * UNITS + u + 1 - XT_RING)
                nc.scalar.activation(
                    xt[:, u % XT_RING, :, 0, :].rearrange("p j (s f) -> p j s f", s=GROUP)[:, :, :, 0:FEATS],
                    turned_ps[:, u % TURN_RING, 0:UNIT_COLS].rearrange("p (j s f) -> p j s f", s=GROUP, f=FEATS),
                    ACT.Copy).then_inc(xt_hi_done, 1)

            def gram_parts(d, u):
                act.wait_ge(gram_done, d * UNITS + u + 1)
                if not (isinstance(d, int) and d == 0 and u < 2):
                    act.wait_ge(grams_done, d * UNITS + u - 1)
                else:
                    act.wait_ge(parts_zeroed, 1)
                b = u % GRAM_RING * GRAM_BANKS
                for s in range(GROUP):
                    quad = slice(QUAD * s, QUAD * s + FEATS)
                    last = nc.scalar.activation(
                        parts[quad, u % 2, :, :, 0:FEATS],
                        gram_ps[quad, b:b + GRAM_BANKS, :].rearrange("p a (b h n) -> p h (a b) n", h=2, n=P)[
                            :, :, :, QUAD * s:QUAD * s + FEATS], ACT.Copy)
                last.then_inc(parts_done, 1)

            def drain(c, layer, m):
                slot = slot_of(layer, m)
                act.wait_ge(filled, slot_count(c, slot))
                if not (isinstance(c, int) and c == 0 and slot < 2):
                    act.wait_ge(split_done, slot_count(c, slot) - 2)
                nc.scalar.activation(h_full[:, slot % 2, :], acc_slot(slot), ACT.Relu,
                                     bias=small_t[:, slot:slot + 1]).then_inc(drained, 1)

            def mlp_hi(d):
                act.wait_ge(mlp_turned, d + 1)
                nc.scalar.activation(cols(x0[:, 0, 0, :]), by_sample(mlp_bank), ACT.Copy).then_inc(mlp_hi_done, 1)

            def pairs_hi(d):
                act.wait_ge(gathered, (d + 1) * 16 * len(PIECES))
                for t in range(3):
                    nc.scalar.activation(x0[:, 1 + t, 0, :], pairs[:, t, :], ACT.Copy).then_inc(pairs_hi_done, 1)

            def out_row(c):
                act.wait_ge(out_filled, c + 1)
                if not (isinstance(c, int) and c == 0):
                    act.wait_ge(y_stored, c * 16)
                nc.scalar.activation(by_sample(y_row[:, :]), cols(out_bank), ACT.Identity,
                                     bias=bout[:, :]).then_inc(out_drained, 1)

            def chunk(c):
                ends = isinstance(c, int) and c == CHUNKS - 1
                for step in chunk_steps(not ends, isinstance(c, int) and c == 0):
                    if step[0] == "mm":
                        _, layer, m, _, k1 = step
                        if k1 == K_TILES[layer]:
                            drain(c, layer, m)
                    elif step[0] == "turn":
                        turned_hi(c + 1, step[1])
                    elif step[0] == "gram":
                        gram_parts(c + 1, step[1])
                    elif step[0] == "weights":
                        weights_hi(step[1])
                    elif step[0] == "mlp":
                        mlp_hi(c + 1)
                    elif step[0] == "pairs":
                        pairs_hi(c + 1)
                    elif step[0] == "out" and not (isinstance(c, int) and c == 0):
                        out_row(c - 1)

            for step in first_steps():
                if step[0] == "turn":
                    turned_hi(0, step[1])
                elif step[0] == "gram":
                    gram_parts(0, step[1])
                elif step[0] == "weights":
                    weights_hi(step[1])
                elif step[0] == "mlp":
                    mlp_hi(0)
                elif step[0] == "pairs":
                    pairs_hi(0)
            chunk(0)
            with act.Fori(1, CHUNKS - 1) as c:
                chunk(c)
            chunk(CHUNKS - 1)
            out_row(CHUNKS - 1)

        @block.vector
        def _(dve):
            def weights_lo(n):
                g, bank = ORDER[n], weight_bank(n)
                dve.wait_ge(w_hi_done, n + 1)
                t = tile_of_group(g)
                if g == W0_GROUPS:
                    last = nc.vector.tensor_scalar(ones[:], ident[:, 0:1], 0.0, 1.0, ALU.mult, ALU.add)
                elif g < W0_GROUPS:
                    a, b = t * P, (t + 3) * P
                    nc.vector.tensor_tensor(w_lo[:, a:b], bank[:, 0:3 * P], w_hi[:, a:b].bitcast(F32), ALU.subtract)
                    a, b = b, b + P
                    last = nc.vector.tensor_tensor(w_lo[0:K_LAST, a:b], bank[0:K_LAST, 3 * P:4 * P],
                                                   w_hi[0:K_LAST, a:b].bitcast(F32), ALU.subtract)
                else:
                    a, b = t * P, (t + 4) * P
                    last = nc.vector.tensor_tensor(w_lo[:, a:b], bank, w_hi[:, a:b].bitcast(F32), ALU.subtract)
                last.then_inc(w_done, 1)

            def turned_lo(d, u):
                dve.wait_ge(xt_hi_done, d * UNITS + u + 1)
                hi, lo = (xt[:, u % XT_RING, :, h, :].rearrange("p j (s f) -> p j s f", s=GROUP)[:, :, :, 0:FEATS]
                          for h in range(2))
                nc.vector.tensor_tensor(
                    lo, turned_ps[:, u % TURN_RING, 0:UNIT_COLS].rearrange("p (j s f) -> p j s f", s=GROUP, f=FEATS),
                    hi.bitcast(F32), ALU.subtract).then_inc(xt_done, 1)

            def gram_low(d, u):
                n = d * UNITS + u + 1
                hh, hl = parts[:, u % 2, 0], parts[:, u % 2, 1]
                dve.wait_ge(parts_done, n)
                if not (isinstance(d, int) and d == 0 and u < 2):
                    dve.wait_ge(grams_done, n - 2)
                if u == 0 and not (isinstance(d, int) and d < 2):
                    dve.wait_ge(summed_done, d - 1)
                nc.vector.transpose(low_t[:, u % 2].rearrange("p j g -> p (j g)"),
                                    hl.rearrange("p j g -> p (j g)")).then_inc(low_turned, 1)
                nc.vector.tensor_tensor(hh, hh, hl, ALU.add).then_inc(sum_done, 1)

            def gram_sum(d, u):
                n = d * UNITS + u + 1
                dve.wait_ge(low_turned, n)
                dve.wait_ge(sum_done, n)
                if not (isinstance(d, int) and d == 0) and u == 0:
                    dve.wait_ge(spilled, d * GROUP * 16)
                nc.vector.tensor_tensor(
                    grams[:, :, u * UNIT_GROUPS:(u + 1) * UNIT_GROUPS].rearrange("p g j -> p j g"),
                    parts[:, u % 2, 0, :, 0:FEATS], low_t[:, u % 2, :, 0:FEATS], ALU.add).then_inc(grams_done, 1)

            def split(c, layer, m):
                slot, h = slot_of(layer, m), h_b if layer == 1 else h_a
                full, high, low = h_full[:, slot % 2, :], h[:, m, 0, :], h[:, m, 1, :]
                dve.wait_ge(drained, slot_count(c, slot))
                nc.vector.tensor_copy(high, full).then_inc(high_done, 1)
                dve.wait_ge(high_done, c * FIRST_SLOT[3] + slot + 1)
                nc.vector.tensor_tensor(low, full, high.bitcast(F32), ALU.subtract).then_inc(split_done, 1)

            def weigh(c, m):
                slot = slot_of(3, m)
                weighted = low_t.rearrange("p r j g -> p (r j g)")
                full, w = h_full[:, slot % 2, :], small_t[:, SLOTS + m:SLOTS + m + 1]
                dve.wait_ge(drained, slot_count(c, slot))
                if m == 0:
                    ends = isinstance(c, int) and c == CHUNKS - 1
                    dve.wait_ge(grams_done, (c + (1 if ends else 2)) * UNITS)
                    nc.vector.tensor_scalar(weighted, full, w, None, ALU.mult).then_inc(split_done, 1)
                    return
                dve.wait_ge(split_done, slot_count(c, slot) - 1)
                nc.vector.scalar_tensor_tensor(weighted, full, w, weighted, ALU.mult,
                                               ALU.add).then_inc(split_done, 1)
                dve.wait_ge(split_done, slot_count(c, slot))
                nc.vector.tensor_copy(h_a[:, 4, 0, :], weighted).then_inc(summed_hi_done, 1)
                dve.wait_ge(summed_hi_done, c + 1)
                nc.vector.tensor_tensor(h_a[:, 4, 1, :], weighted, h_a[:, 4, 0, :].bitcast(F32),
                                        ALU.subtract).then_inc(summed_done, 1)

            def mlp_lo(d):
                dve.wait_ge(mlp_hi_done, d + 1)
                nc.vector.tensor_tensor(cols(x0[:, 0, 1, :]), by_sample(mlp_bank), cols(x0[:, 0, 0, :].bitcast(F32)),
                                        ALU.subtract).then_inc(mlp_done, 1)

            def pairs_lo(d):
                for t in range(3):
                    dve.wait_ge(pairs_hi_done, d * 3 + t + 1)
                    nc.vector.tensor_tensor(x0[:, 1 + t, 1, :], pairs[:, t, :], x0[:, 1 + t, 0, :].bitcast(F32),
                                            ALU.subtract).then_inc(pairs_done, 1)

            def chunk(c):
                ends = isinstance(c, int) and c == CHUNKS - 1
                for step in chunk_steps(not ends, isinstance(c, int) and c == 0):
                    if step[0] == "mm":
                        _, layer, m, _, k1 = step
                        if k1 == K_TILES[layer]:
                            if layer < 3:
                                split(c, layer, m)
                            else:
                                weigh(c, m)
                    elif step[0] == "turn":
                        turned_lo(c + 1, step[1])
                    elif step[0] == "gram":
                        gram_low(c + 1, step[1])
                    elif step[0] == "sum":
                        gram_sum(c + 1, step[1])
                    elif step[0] == "weights":
                        weights_lo(step[1])
                    elif step[0] == "mlp":
                        mlp_lo(c + 1)
                    elif step[0] == "pairs":
                        pairs_lo(c + 1)

            nc.vector.memset(xt[:].bitcast(F32).rearrange("p r j h (s f) -> p (r j h s) f", f=QUAD)[:, :, FEATS:],
                             0.0).then_inc(xt_zeroed, 1)
            nc.vector.memset(parts[:], 0.0).then_inc(parts_zeroed, 1)
            for step in first_steps():
                if step[0] == "turn":
                    turned_lo(0, step[1])
                elif step[0] == "gram":
                    gram_low(0, step[1])
                elif step[0] == "sum":
                    gram_sum(0, step[1])
                elif step[0] == "weights":
                    weights_lo(step[1])
                elif step[0] == "mlp":
                    mlp_lo(0)
                elif step[0] == "pairs":
                    pairs_lo(0)
            chunk(0)
            with dve.Fori(1, CHUNKS - 1) as c:
                chunk(c)
            chunk(CHUNKS - 1)


_INS = ['r_bottom_output', 'r_bottom_mlp_output', 'L0_rec_w0', 'L0_rec_b0', 'L0_rec_w1', 'L0_rec_b1', 'L0_rec_w2',
        'L0_rec_b2', 'L0_rec_w3', 'L0_rec_b3', 'L0_rec_w_out', 'L0_rec_b_out']
_OUTS = [((2048, 1), 'float32')]


def kernel(**inputs):
    import numpy as _np
    import concourse.bacc as _bacc
    from concourse import mybir as _mybir
    from concourse.bass_utils import run_bass_kernel_spmd as _run

    nc = _bacc.Bacc("TRN2", target_bir_lowering=False, num_devices=1, dynamic_dma_scratch_size=2048)
    arrays, args = {}, []
    for name in _INS:
        a = _np.ascontiguousarray(inputs[name])
        arrays[f"in_{name}_dram"] = a
        args.append(nc.dram_tensor(f"in_{name}_dram", a.shape, _mybir.dt.from_np(a.dtype), kind="ExternalInput").ap())
    for i, (shape, dtype) in enumerate(_OUTS):
        dt = _mybir.dt.from_np(_np.dtype(dtype))
        args.append(nc.dram_tensor(f"out_{i}_dram", shape, dt, kind="ExternalOutput").ap())
    dlrm_program(nc, *args)
    r = _run(nc, [arrays], core_ids=[0])
    return r.results[0]["out_0_dram"]
```
